# Optimizing a Trainium2 kernel written in Bass

```python
import numpy as np
import jax
import jax.numpy as jnp

def _softmax(x, axis=-1):
    return jax.nn.softmax(x, axis=axis)

def _gelu(x):
    return jax.nn.gelu(x, approximate=True)

def _silu(x):
    return jax.nn.silu(x)

def _sigmoid(x):
    return jax.nn.sigmoid(x)

def _layernorm(x, axis=-1, eps=1e-05):
    m = jnp.mean(x, axis=axis, keepdims=True)
    v = jnp.var(x, axis=axis, keepdims=True)
    return (x - m) / jnp.sqrt(v + eps)

def _scatter_add(tgt, idx, src, axis=0):
    return tgt.at[idx].add(src)

def _segment_sum(src, seg, n):
    return jax.ops.segment_sum(src, seg, n)
kernel_name = 'mk_adj_resnorm_d2_adj_r2_d00fdb'

def setup_inputs(seed: int=0):
    np.random.seed(seed)
    _w = jnp.asarray

    def _rec_inputs():
        import jax
        import jax.numpy as jnp
        _gk = jax.random.key(seed)
        x = -0.0005207 + 1.001 * jax.random.normal(jax.random.fold_in(_gk, 1), (8192, 128), jnp.float32)
        _a = jax.random.bernoulli(jax.random.fold_in(_gk, 2), 0.000488281, (8192, 8192))
        _a = jnp.logical_or(_a, jnp.swapaxes(_a, -1, -2))
        _a = jnp.logical_or(_a, jnp.eye(8192, dtype=bool))
        _af = _a.astype(jnp.float32)
        _af = _af * jax.random.uniform(jax.random.fold_in(_gk, 3), (8192, 8192), jnp.float32, 0.05, 1)
        adj = _af
        return (x, adj)
    x, adj = _rec_inputs()

    def _L0_gnn_setup():
        import jax, jax.numpy as jnp
        import numpy as np
        N = 4096
        D = 128
        L = 2
        key = jax.random.key(seed)
        kz, ka, kw, kb = jax.random.split(key, 4)
        z = jax.random.normal(kz, (N, D), dtype=jnp.float32)
        adj_mat = jax.random.uniform(ka, (N, N), dtype=jnp.float32)
        degree = adj_mat.sum(axis=1)
        W_stack = jax.random.normal(kw, (L, D, D), dtype=jnp.float32)
        B_stack = jax.random.normal(kb, (L, D, D), dtype=jnp.float32)
        return {'z': z, 'adj_mat': adj_mat, 'degree': degree, 'W_stack': W_stack, 'B_stack': B_stack}
    _L0_gnn_all = _L0_gnn_setup()
    _L0_gnn_in = {k: v for k, v in _L0_gnn_all.items() if k in ('W_stack', 'B_stack')}
    del _L0_gnn_all

    def _L1_gnn_setup():
        import jax, jax.numpy as jnp
        import numpy as np
        N = 4096
        D = 128
        CUTOFF = 1.0
        MU = 1.0
        SIGMA = 0.5

        def sensitivity(r, mu, sigma):
            return jnp.exp(-(1.0 / r - 1.0 / mu) ** 2 / (2.0 * sigma * sigma))
        key = jax.random.key(seed)
        k_z, k_d, k_w = jax.random.split(key, 3)
        z = jax.random.normal(k_z, (N, D), dtype=jnp.float32)
        dist_matrix = jax.random.uniform(k_d, (N, N), dtype=jnp.float32) * 2.0 + 0.05
        W = jax.random.normal(k_w, (D, D), dtype=jnp.float32)
        B = jnp.zeros((D,), dtype=jnp.float32)
        return {'z': z, 'dist_matrix': dist_matrix, 'W': W, 'B': B}
    _L1_gnn_all = _L1_gnn_setup()
    _L1_gnn_in = {k: v for k, v in _L1_gnn_all.items() if k in ('W', 'B')}
    del _L1_gnn_all
    return {'x': x, 'adj': adj, 'L0_gnn_W_stack': _L0_gnn_in['W_stack'], 'L0_gnn_B_stack': _L0_gnn_in['B_stack'], 'L1_gnn_W': _L1_gnn_in['W'], 'L1_gnn_B': _L1_gnn_in['B']}

def reference(x, adj, L0_gnn_W_stack, L0_gnn_B_stack, L1_gnn_W, L1_gnn_B):
    import jax
    import jax.numpy as jnp

    def _L0_gnn_ref(z, adj_mat, degree, W_stack, B_stack):
        import jax, jax.numpy as jnp
        import numpy as np
        N = 4096
        D = 128
        L = 2
        inv_deg = (1.0 / degree)[:, None]
        for i in range(W_stack.shape[0]):
            agg = adj_mat @ z * inv_deg
            z = jnp.tanh(agg @ W_stack[i] + z @ B_stack[i])
        return z

    def _L1_gnn_ref(z, dist_matrix, W, B):
        import jax, jax.numpy as jnp
        import numpy as np
        N = 4096
        D = 128
        CUTOFF = 1.0
        MU = 1.0
        SIGMA = 0.5

        def sensitivity(r, mu, sigma):
            return jnp.exp(-(1.0 / r - 1.0 / mu) ** 2 / (2.0 * sigma * sigma))
        msg = z @ W + B
        sens = sensitivity(dist_matrix, MU, SIGMA)
        weights = jnp.where(dist_matrix < CUTOFF, sens, 0.0)
        return weights @ msg
    deg = jnp.maximum((adj != 0).astype(jnp.float32).sum(-1), 1.0)
    x = _layernorm(x + _L0_gnn_ref(x, adj, deg, L0_gnn_W_stack, L0_gnn_B_stack), axis=-1)
    x = _layernorm(x + _L1_gnn_ref(x, adj, L1_gnn_W, L1_gnn_B), axis=-1)
    return x

_drawn_inputs = setup_inputs


def setup_inputs(seed=0):
    import zlib

    import numpy as np

    out = dict(_drawn_inputs(seed))
    spreads = {'L1_gnn_B': (0.0, 0.429)}
    factors = {}
    for name, (base, spread) in spreads.items():
        noise = np.random.default_rng([zlib.crc32(name.encode()), seed]).standard_normal(out[name].shape)
        drawn = base * np.exp(spread * noise) if base else spread * noise
        out[name] = jnp.asarray(drawn.astype(out[name].dtype))
    for name, factor in factors.items():
        out[name] = (out[name] * factor).astype(out[name].dtype)
    return out
```

```python
from contextlib import ExitStack

import concourse.bass as bass
from concourse import mybir

P = 128
D = 128
ROW = 512
T = ROW // P
RING = 4
BAND = 4
EPS = 1e-5
TINY = 1e-15


class Pass:

    def __init__(self, bands):
        self.bands = bands
        self.sums = [[b for b in blocks if b[2]] for blocks in bands]
        self.total = BAND * sum(map(len, bands))
        self.total_sums = BAND * sum(map(len, self.sums))

    def before(self, band, i):
        return BAND * sum(map(len, self.bands[:band])) + i * len(self.bands[band])

    def sums_before(self, band, i):
        return BAND * sum(map(len, self.sums[:band])) + i * len(self.sums[band])


def passes(groups):
    lows = range(0, groups, BAND)
    up = [[(g, g < lo, False) for g in [*range(lo, groups), *range(lo)]] for lo in lows]
    down = [[(g, True, False) for g in range(lo, lo + BAND)]
            + [(g, True, True) for g in range(groups - 1, lo + BAND - 1, -1)] for lo in reversed(lows)]
    rest = [[(g, False, True) for g in range(lo + BAND - 1, -1, -1)] for lo in reversed(lows)]
    return Pass(up), Pass(down), Pass(rest)


def each_row(engine, table, row, peeled=1):
    for band in range(len(table.bands)):
        first = 0
        if band < peeled:
            row(band, 0, band * BAND)
            first = 1
        with engine.Fori(first, BAND) as i:
            row(band, i, i + band * BAND)


class Steps:

    def __init__(self, engine, sem, base):
        self.engine, self.sem, self.base, self.n = engine, sem, base, 0

    def did(self, instruction):
        self.n += 1
        return instruction.then_inc(self.sem, 1)

    def settle(self):
        self.engine.wait_ge(self.sem, self.base + self.n)


def graph_kernel(nc: bass.Bass, x, x_t, adj, w_stack, b_stack, w_msg, bias_msg, out):
    dt = mybir.dt
    f32, bf16, u32 = dt.float32, dt.bfloat16, dt.uint32
    ALU, ACT = mybir.AluOpType, mybir.ActivationFunctionType

    G = x.shape[0] // ROW
    A, B, C = passes(G)
    LAST_A, LAST_B, LAST_C = (len(t.bands) - 1 for t in (A, B, C))

    inv_deg_d = nc.dram_tensor("inv_deg_d", (G, P, ROW), f32, kind="Internal").ap()
    agg_d = nc.dram_tensor("agg_d", (G, P, ROW), f32, kind="Internal").ap()
    z1t_d = nc.dram_tensor("z1t_d", (G, P, ROW), f32, kind="Internal").ap()
    sum_d = nc.dram_tensor("sum_d", (G, P, ROW), f32, kind="Internal").ap()
    x1_d = nc.dram_tensor("x1_d", (G, P, T, D), f32, kind="Internal").ap()

    x_rows = x.rearrange("(c t p) d -> c p t d", t=T, p=P)
    out_rows = out.rearrange("(c t p) d -> c p t d", t=T, p=P)
    x_tiles = x.rearrange("(g p) d -> p g d", p=P)
    x_t_rows = x_t.rearrange("d (c n) -> c d n", n=ROW)

    ctx = ExitStack()
    with ctx:
        def sb(name, shape, dtype=f32):
            return ctx.enter_context(nc.sbuf_tensor(name, shape, dtype))

        def pb(name, shape):
            return ctx.enter_context(nc.psum_tensor(name, shape, f32))

        def sem(name):
            return ctx.enter_context(nc.semaphore(name))

        x_msg = sb("x_msg", [P, G * T, D])
        z1_nat = sb("z1_nat", [P, G * T, D])
        ring = sb("ring", [P, RING, T, ROW])
        masked = sb("masked", [P, 2, T * ROW])
        logs = sb("logs", [P, 4, T * ROW])
        weights = sb("weights", [P, 2, T * ROW])
        nonzero = sb("nonzero", [P, 2, T * ROW], bf16)
        ones_b = sb("ones_b", [P, P], bf16)
        ones_row = sb("ones_row", [1, P])
        ident = sb("ident", [P, P])
        w0, w1, b0, b1, wm = (sb(n, [P, D]) for n in ("w0", "w1", "b0", "b1", "wm"))
        bias_row = sb("bias_row", [1, D])
        tiny_c = sb("tiny_c", [P, 1])
        minus2_c = sb("minus2_c", [P, 1])
        inv_t = sb("inv_t", [P, ROW])
        deg_t = sb("deg_t", [P, ROW])
        part_t = sb("part_t", [P, ROW])
        agg_t = sb("agg_t", [P, ROW])
        side_t = sb("side_t", [P, ROW])
        tanh_t = sb("tanh_t", [P, ROW])
        sum_t = sb("sum_t", [P, ROW])
        res_t = sb("res_t", [P, T, D])
        pre_t = sb("pre_t", [P, T, D])
        norm_t = sb("norm_t", [P, T, D])
        x1t_t = sb("x1t_t", [P, T, P])
        stats = sb("stats", [P, T, 6])
        mean_var = sb("mean_var", [P, T, 2])
        var_eps, ln_var, rstd0, newton, rstd = (
            sb(n, [P, T]) for n in ("var_eps", "ln_var", "rstd0", "newton", "rstd"))

        acc_p = pb("acc_p", [P, 2, ROW])
        acc_q = pb("acc_q", [P, 2, ROW])
        deg_p = pb("deg_p", [P, ROW])
        pre_p = pb("pre_p", [P, ROW])
        turn_p = pb("turn_p", [P, T, P])
        msg_p = pb("msg_p", [P, T, D])

        consts_in, x_in, consts_set, ident_set = map(sem, ("consts_in", "x_in", "consts_set", "ident_set"))
        adj_in = [sem(f"adj_in{k}") for k in range(RING)]
        adj_pe = sem("adj_pe")
        adj_dve = sem("adj_dve")
        abs_done, ln_done, square_done = map(sem, ("abs_done", "ln_done", "square_done"))
        exponent_done, weight_done = map(sem, ("exponent_done", "weight_done"))
        weight_read = sem("weight_read")
        ta_pe, ta_dve, ta_act = map(sem, ("ta_pe", "ta_dve", "ta_act"))
        tb_pe, tb_dve, tb_act = map(sem, ("tb_pe", "tb_dve", "tb_act"))
        tc_pe, tc_dve, tc_act = map(sem, ("tc_pe", "tc_dve", "tc_act"))
        side_a, side_b, side_c = map(sem, ("side_a", "side_b", "side_c"))
        kept_inv, kept_agg, kept_z1, kept_sum, kept_x1, kept_out = map(
            sem, ("kept_inv", "kept_agg", "kept_z1", "kept_sum", "kept_x1", "kept_out"))

        A_PE, A_DVE, A_ACT = 3, 5, 1
        A_AGG, A_Z1 = 4, 5
        NORM = 1 + T + T + 1
        FINISH = 3 + T
        B_PE, B_ACT = 4, 3
        B_AGG, B_VAR = 3, 3 + NORM
        B_X1 = B_VAR + 1 + FINISH
        B_X1T, B_MSG = B_X1 + 1, B_X1 + 2
        B_DVE = B_MSG
        C_PE, C_ACT = 1, 2
        C_SUM, C_VAR = 1, 1 + NORM
        C_OUT = C_DVE = C_VAR + 1 + FINISH

        def apart(engine):
            engine.sem_inc(passed[engine], 1)

        def landed(table, loads_before, band, i, k):
            in_slot = loads_before // RING + table.before(band, 0) // RING + k // RING + 1
            return 16 * (i * (len(table.bands[band]) // RING) + in_slot)

        passed = {nc.sync: sem("passed_sp"), nc.gpsimd: sem("passed_pool"), nc.vector: sem("passed_dve")}

        block = ctx.enter_context(nc.Block())

        @block.sync
        def _(sp):
            quarter = G * T // 4

            def load(k, c, g):
                sp.dma_start(ring[:, k % RING, :, :], adj[c, g]).then_inc(adj_in[k % RING], 16)

            for tile, src in ((w0, w_stack[0]), (b0, b_stack[0]), (w1, w_stack[1]),
                              (b1, b_stack[1]), (wm, w_msg), (bias_row, bias_msg)):
                sp.dma_start(tile[:, :], src).then_inc(consts_in, 16)

            def load_row_a(band, i, r):
                for k, (g, _, _) in enumerate(A.bands[band]):
                    n = A.before(band, i) + k
                    if not (isinstance(n, int) and n < RING):
                        sp.wait_ge(adj_pe, n - RING + 1)
                        sp.wait_ge(adj_dve, n - RING + 1)
                    apart(sp)
                    load(k, r, g)
                    if isinstance(n, int) and n < 4:
                        tiles = slice(n * quarter, (n + 1) * quarter)
                        sp.dma_start(x_msg[:, tiles, :], x_tiles[:, tiles, :]).then_inc(x_in, 16)

            def load_row_b(band, i, r):
                summed = B.sums_before(band, i)
                for k, (g, _, _) in enumerate(B.bands[band]):
                    sp.wait_ge(adj_pe, A.total + B.before(band, i) + k - RING + 1)
                    apart(sp)
                    if band == 0:
                        seen = A.total - RING + 1 + k if isinstance(i, int) else A.total
                    elif k < RING:
                        seen = A.total + summed - (RING - 1 - k if band > 1 or not isinstance(i, int) else 0)
                    else:
                        seen = A.total + summed + max(0, k - RING - BAND + 1)
                    sp.wait_ge(adj_dve, seen)
                    apart(sp)
                    load(k, G - 1 - r, g)

            def load_row_c(band, i, r):
                for k, (g, _, _) in enumerate(C.bands[band]):
                    l = B.total_sums + C.sums_before(band, i) + k
                    if isinstance(l, int):
                        sp.wait_ge(adj_pe, min(A.total + B.total, A.total + B.total - RING + 1 + k))
                    sp.wait_ge(adj_dve, A.total + l - RING + 1)
                    apart(sp)
                    load(k, G - 1 - r, g)

            each_row(sp, A, load_row_a)
            each_row(sp, B, load_row_b, peeled=2)
            each_row(sp, C, load_row_c)

        @block.gpsimd
        def _(pool):
            pool.memset(ident[:, :], 0.0).then_inc(ident_set, 1)
            pool.wait_ge(ident_set, 1)
            pool.affine_select(out=ident[:, :], in_=ident[:, :], compare_op=ALU.not_equal, fill=1.0,
                               base=0, pattern=[[-1, P]], channel_multiplier=1).then_inc(ident_set, 1)

            def side_row_a(c):
                if not (isinstance(c, int) and c == 0):
                    pool.wait_ge(ta_pe, c * A_PE)
                apart(pool)
                pool.dma_start(side_t[:, :], x_t_rows[c]).then_inc(side_a, 16)
                pool.wait_ge(ta_dve, c * A_DVE + A_AGG)
                apart(pool)
                pool.dma_start(inv_deg_d[c], inv_t[:, :]).then_inc(kept_inv, 16)
                pool.dma_start(agg_d[c], part_t[:, :]).then_inc(kept_agg, 16)
                pool.wait_ge(ta_act, c * A_ACT + 1)
                apart(pool)
                pool.dma_start(z1t_d[c], tanh_t[:, :]).then_inc(kept_z1, 16)

            def side_row_b(r):
                c = G - 1 - r
                if isinstance(r, int) and r == 0:
                    pool.wait_ge(ta_dve, G * A_DVE)
                    pool.wait_ge(kept_inv, 16 * G)
                    pool.wait_ge(kept_agg, 16 * G)
                    pool.wait_ge(kept_z1, 16 * G)
                else:
                    pool.wait_ge(tb_dve, r * B_DVE)
                    pool.wait_ge(kept_x1, r * 16)
                apart(pool)
                pool.dma_start(inv_t[:, :], inv_deg_d[c]).then_inc(side_b, 16)
                pool.dma_start(part_t[:, :], agg_d[c]).then_inc(side_b, 16)
                pool.dma_start(side_t[:, :], z1t_d[c]).then_inc(side_b, 16)
                pool.dma_start(res_t[:, :, :], x_rows[c]).then_inc(side_b, 16)
                pool.wait_ge(tb_dve, r * B_DVE + 1)
                apart(pool)
                pool.dma_start(sum_d[c], sum_t[:, :]).then_inc(kept_sum, 16)
                pool.wait_ge(tb_dve, r * B_DVE + B_X1)
                apart(pool)
                pool.dma_start(x1_d[c], norm_t[:, :, :]).then_inc(kept_x1, 16)

            def side_row_c(r):
                c = G - 1 - r
                if isinstance(r, int) and r == 0:
                    pool.wait_ge(tb_dve, G * B_DVE)
                    pool.wait_ge(kept_sum, 16 * G)
                    pool.wait_ge(kept_x1, 16 * G)
                else:
                    pool.wait_ge(tc_dve, r * C_DVE)
                apart(pool)
                pool.dma_start(part_t[:, :], sum_d[c]).then_inc(side_c, 16)
                pool.dma_start(res_t[:, :, :], x1_d[c]).then_inc(side_c, 16)
                pool.wait_ge(tc_dve, r * C_DVE + C_OUT)
                apart(pool)
                pool.dma_start(out_rows[c], norm_t[:, :, :]).then_inc(kept_out, 16)

            for side_row in (side_row_a, side_row_b, side_row_c):
                side_row(0)
                with pool.Fori(1, G) as r:
                    side_row(r)
            pool.wait_ge(kept_out, 16 * G)

        @block.tensor
        def _(pe):
            def product(acc, stationary, moving, first, last):
                for t in range(T):
                    mm = pe.matmul(acc, stationary[:, t, :], moving[:, t, :],
                                   start=first and t == 0, stop=last and t == T - 1)
                return mm

            def tiles(z, g):
                return z[:, g * T:(g + 1) * T, :]

            def turn(steps, src):
                for t in range(T):
                    mm = pe.transpose(turn_p[:, t, :], src[:, t, :], ident[:, :])
                steps.did(mm)

            def tail_a(c):
                steps = Steps(pe, ta_pe, c * A_PE)

                def degree():
                    pe.wait_ge(adj_dve, (c + 1) * G)
                    for t in range(T):
                        mm = pe.matmul(deg_p[:, :], ones_b[:, :], nonzero[:, c % 2, t * ROW:(t + 1) * ROW],
                                       start=t == 0, stop=t == T - 1)
                    steps.did(mm)

                def layer():
                    pe.wait_ge(ta_dve, c * A_DVE + A_AGG)
                    pe.wait_ge(side_a, (c + 1) * 16)
                    pe.matmul(pre_p[:, :], w0[:, :], agg_t[:, :], start=True, stop=False)
                    steps.did(pe.matmul(pre_p[:, :], b0[:, :], side_t[:, :], start=False, stop=True))

                def turn_z1():
                    pe.wait_ge(ta_act, c * A_ACT + 1)
                    turn(steps, tanh_t[:, :].rearrange("d (t p) -> d t p", p=P))

                return degree, layer, turn_z1

            def tail_b(r):
                steps = Steps(pe, tb_pe, r * B_PE)

                def layer():
                    pe.wait_ge(tb_dve, r * B_DVE + B_AGG)
                    pe.wait_ge(side_b, (r + 1) * 64)
                    pe.matmul(pre_p[:, :], w1[:, :], agg_t[:, :], start=True, stop=False)
                    steps.did(pe.matmul(pre_p[:, :], b1[:, :], side_t[:, :], start=False, stop=True))

                def turn_z2():
                    pe.wait_ge(tb_act, r * B_ACT + 1)
                    turn(steps, tanh_t[:, :].rearrange("d (t p) -> d t p", p=P))

                def turn_x1():
                    pe.wait_ge(tb_dve, r * B_DVE + B_X1)
                    turn(steps, norm_t)

                def messages():
                    pe.wait_ge(tb_dve, r * B_DVE + B_X1T)
                    for t in range(T):
                        pe.matmul(msg_p[:, t, :], x1t_t[:, t, :], wm[:, :], start=True, stop=False)
                        mm = pe.matmul(msg_p[:, t, :], ones_row[:, :], bias_row[:, :], start=False, stop=True)
                    steps.did(mm)

                return layer, turn_z2, turn_x1, messages

            def tail_c(r):
                steps = Steps(pe, tc_pe, r * C_PE)

                def turn_sum():
                    pe.wait_ge(tc_dve, r * C_DVE + C_SUM)
                    turn(steps, sum_t[:, :].rearrange("d (t p) -> d t p", p=P))

                return (turn_sum,)

            def row_of_a(band, i, r):
                blocks = A.bands[band]
                degree, layer, turn_z1 = tail_a(r - 1)
                tail = not (isinstance(r, int) and r == 0)
                if tail:
                    degree()
                for k, (g, second, _) in enumerate(blocks):
                    if isinstance(r, int) and r == 0 and k % (G // 4) == 0:
                        pe.wait_ge(x_in, 64)
                    pe.wait_ge(adj_in[k % RING], landed(A, 0, band, i, k))
                    mm = product(acc_p[:, r % 2, :], tiles(x_msg, g), ring[:, k % RING], k == 0, k == G - 1)
                    if second:
                        pe.wait_ge(ta_dve, (g + 1) * A_DVE)
                        mm = product(acc_q[:, r % 2, :], tiles(z1_nat, g), ring[:, k % RING],
                                     g == 0, k == G - 1)
                    mm.then_inc(adj_pe, 1)
                    if tail and k == 1:
                        layer()
                    if tail and k == 2:
                        turn_z1()

            def row_of_b(band, i, r):
                blocks = B.bands[band]
                tail = () if isinstance(r, int) and r == 0 else tail_b(r - 1)
                places = [0, 1, 3, min(4, len(blocks) - 1)]
                l = B.sums_before(band, i)
                summed = 0
                for k, (g, _, in_sum) in enumerate(blocks):
                    pe.wait_ge(adj_in[k % RING], landed(B, A.total, band, i, k))
                    pe.wait_ge(ta_dve, (g + 1) * A_DVE)
                    mm = product(acc_p[:, r % 2, :], tiles(z1_nat, g), ring[:, k % RING],
                                 k == 0, k == len(blocks) - 1)
                    mm.then_inc(adj_pe, 1)
                    if in_sum:
                        pe.wait_ge(tb_dve, (G - g) * B_DVE)
                        pe.wait_ge(weight_done, l + summed + 1)
                        mm = product(acc_q[:, r % 2, :], tiles(x_msg, g),
                                     weights[:, summed % 2, :].rearrange("p (t n) -> p t n", t=T),
                                     summed == 0, k == len(blocks) - 1)
                        mm.then_inc(weight_read, 1)
                        summed += 1
                    for step, place in zip(tail, places):
                        if place == k:
                            step()

            def row_of_c(band, i, r):
                blocks = C.bands[band]
                if isinstance(r, int) and r == 0:
                    tail, places = tail_b(G - 1), (-1, -1, 1, 2)
                else:
                    tail, places = tail_c(r - 1), (0,)
                l = B.total_sums + C.sums_before(band, i)
                for step, place in zip(tail, places):
                    if place < 0:
                        step()
                for k, (g, _, _) in enumerate(blocks):
                    if isinstance(r, int) and r == 0:
                        pe.wait_ge(tb_dve, (G - g) * B_DVE)
                    pe.wait_ge(weight_done, l + k + 1)
                    mm = product(acc_p[:, r % 2, :], tiles(x_msg, g),
                                 weights[:, k % 2, :].rearrange("p (t n) -> p t n", t=T),
                                 k == 0, k == len(blocks) - 1)
                    mm.then_inc(weight_read, 1)
                    for step, place in zip(tail, places):
                        if place == k:
                            step()

            pe.wait_ge(consts_in, 6 * 16)
            pe.wait_ge(consts_set, 4)
            pe.wait_ge(ident_set, 2)
            each_row(pe, A, row_of_a)
            for step in tail_a(G - 1):
                step()
            each_row(pe, B, row_of_b, peeled=2)
            each_row(pe, C, row_of_c)
            for step in tail_c(G - 1):
                step()

        @block.vector
        def _(dve):
            def norm_stats(steps, pe_sem, pe_value, side_sem, side_value):
                dve.wait_ge(pe_sem, pe_value)
                dve.wait_ge(side_sem, side_value)
                steps.did(dve.tensor_tensor(out=pre_t[:, :, :], in0=turn_p[:, :, :], in1=res_t[:, :, :], op=ALU.add))
                steps.settle()
                for t in range(T):
                    steps.did(dve.bn_stats(out=stats[:, t, :], in_=pre_t[:, t, :]))
                steps.settle()
                apart(dve)
                for t in range(T):
                    steps.did(dve.bn_aggr(out=mean_var[:, t, :], in_=stats[:, t, :]))
                steps.settle()
                steps.did(dve.tensor_scalar(var_eps[:, :], mean_var[:, :, 1], EPS, None, ALU.add))

            def norm_finish(steps, act_sem, act_value, kept, kept_value):
                dve.wait_ge(act_sem, act_value)
                steps.did(dve.tensor_tensor(out=newton[:, :], in0=rstd0[:, :], in1=rstd0[:, :], op=ALU.mult))
                steps.settle()
                steps.did(dve.tensor_tensor(out=newton[:, :], in0=newton[:, :], in1=var_eps[:, :], op=ALU.mult))
                steps.settle()
                steps.did(dve.tensor_scalar(newton[:, :], newton[:, :], -0.5, 1.5, ALU.mult, ALU.add))
                steps.settle()
                steps.did(dve.tensor_tensor(out=rstd[:, :], in0=newton[:, :], in1=rstd0[:, :], op=ALU.mult))
                steps.settle()
                if kept_value is not None:
                    dve.wait_ge(kept, kept_value)
                for t in range(T):
                    steps.did(dve.tensor_scalar(norm_t[:, t, :], pre_t[:, t, :], mean_var[:, t, 0:1],
                                                rstd[:, t:t + 1], ALU.subtract, ALU.mult))

            def tail_a(c, partial):
                steps = Steps(dve, ta_dve, c * A_DVE)
                first = isinstance(c, int) and c == 0

                def aggregate():
                    dve.wait_ge(ta_pe, c * A_PE + 1)
                    dve.wait_ge(adj_pe, (c + 1) * G)
                    if not first:
                        dve.wait_ge(kept_inv, c * 16)
                        dve.wait_ge(kept_agg, c * 16)
                    steps.did(dve.tensor_scalar(deg_t[:, :], deg_p[:, :], 1.0, None, ALU.max))
                    if partial:
                        steps.did(dve.tensor_copy(part_t[:, :], acc_q[:, c % 2, :]))
                    else:
                        steps.did(dve.memset(part_t[:, :], 0.0))
                    steps.settle()
                    steps.did(dve.reciprocal(inv_t[:, :], deg_t[:, :]))
                    steps.settle()
                    steps.did(dve.tensor_tensor(out=agg_t[:, :], in0=acc_p[:, c % 2, :], in1=inv_t[:, :], op=ALU.mult))

                def keep_z1():
                    dve.wait_ge(ta_pe, c * A_PE + 3)
                    apart(dve)
                    steps.did(dve.tensor_copy(z1_nat[:, bass.ds(c * T, T), :], turn_p[:, :, :]))

                return aggregate, keep_z1

            def tail_b(r, partial, blocks, summed):
                steps = Steps(dve, tb_dve, r * B_DVE)
                first = isinstance(r, int) and r == 0

                def aggregate():
                    dve.wait_ge(adj_pe, A.total + blocks)
                    if partial:
                        dve.wait_ge(weight_read, summed)
                    if not first:
                        dve.wait_ge(kept_sum, r * 16)
                    if partial:
                        steps.did(dve.tensor_copy(sum_t[:, :], acc_q[:, r % 2, :]))
                    else:
                        steps.did(dve.memset(sum_t[:, :], 0.0))
                    dve.wait_ge(side_b, (r + 1) * 64)
                    steps.did(dve.tensor_tensor(out=agg_t[:, :], in0=acc_p[:, r % 2, :], in1=part_t[:, :], op=ALU.add))
                    steps.settle()
                    steps.did(dve.tensor_tensor(out=agg_t[:, :], in0=agg_t[:, :], in1=inv_t[:, :], op=ALU.mult))

                def norm_in():
                    norm_stats(steps, tb_pe, r * B_PE + 2, side_b, (r + 1) * 64)

                def norm_out():
                    norm_finish(steps, tb_act, r * B_ACT + 3, kept_x1, None if first else r * 16)

                def keep_x1t():
                    dve.wait_ge(tb_pe, r * B_PE + 3)
                    steps.did(dve.tensor_copy(x1t_t[:, :, :], turn_p[:, :, :]))

                def keep_messages():
                    dve.wait_ge(tb_pe, r * B_PE + 4)
                    apart(dve)
                    steps.did(dve.tensor_copy(x_msg[:, bass.ds((G - 1 - r) * T, T), :], msg_p[:, :, :]))
                    assert steps.n == B_DVE

                return aggregate, norm_in, norm_out, keep_x1t, keep_messages

            def tail_c(r, summed):
                steps = Steps(dve, tc_dve, r * C_DVE)
                first = isinstance(r, int) and r == 0

                def whole_sum():
                    dve.wait_ge(weight_read, summed)
                    dve.wait_ge(side_c, (r + 1) * 32)
                    if first:
                        dve.wait_ge(kept_sum, G * 16)
                    steps.did(dve.tensor_tensor(out=sum_t[:, :], in0=acc_p[:, r % 2, :], in1=part_t[:, :], op=ALU.add))

                def norm_in():
                    norm_stats(steps, tc_pe, r * C_PE + 1, side_c, (r + 1) * 32)

                def norm_out():
                    norm_finish(steps, tc_act, r * C_ACT + 2, kept_x1 if first else kept_out,
                                G * 16 if first else r * 16)
                    assert steps.n == C_DVE

                return whole_sum, norm_in, norm_out

            def mask(l, slot, buf, in_value):
                dve.wait_ge(adj_in[slot], in_value)
                if not (isinstance(l, int) and l < 2):
                    dve.wait_ge(exponent_done, l - 1)
                r = ring[:, slot].rearrange("p t n -> p (t n)")
                dve.scalar_tensor_tensor(out=masked[:, buf % 2, :], in0=r, scalar=1.0, in1=r,
                                         op0=ALU.is_lt, op1=ALU.mult).then_inc(adj_dve, 1)
                dve.wait_ge(adj_dve, A.total + l + 1)
                if not (isinstance(l, int) and l < 4):
                    dve.wait_ge(weight_done, l - 3)
                dve.tensor_scalar(logs[:, buf, :].bitcast(u32), masked[:, buf % 2, :].bitcast(u32), 0x7FFFFFFF,
                                  None, ALU.bitwise_and).then_inc(abs_done, 1)

            def exponent(l, buf):
                dve.wait_ge(square_done, l + 1)
                dve.scalar_tensor_tensor(out=logs[:, buf, :], in0=masked[:, buf % 2, :], scalar=-0.5,
                                         in1=logs[:, buf, :], op0=ALU.add, op1=ALU.mult
                                         ).then_inc(exponent_done, 1)

            def row_of_a(band, i, r):
                tail = not (isinstance(r, int) and r == 0)
                aggregate, keep_z1 = tail_a(r - 1, band > 0 and not (band == 1 and isinstance(i, int)))
                for k in range(G):
                    n = A.before(band, i) + k
                    dve.wait_ge(adj_in[k % RING], landed(A, 0, band, i, k))
                    seen = ring[:, k % RING].rearrange("p t n -> p (t n)")
                    counts = nonzero[:, r % 2, :]
                    if k == 0:
                        dve.tensor_scalar(counts, seen, 0.0, None, ALU.not_equal).then_inc(adj_dve, 1)
                    else:
                        dve.wait_ge(adj_dve, n)
                        dve.scalar_tensor_tensor(out=counts, in0=seen, scalar=0.0, in1=counts,
                                                 op0=ALU.not_equal, op1=ALU.add).then_inc(adj_dve, 1)
                    if tail and k == 1:
                        aggregate()
                    if tail and k == 3:
                        keep_z1()

            def row_of_b(band, i, r):
                tail = []
                l = B.sums_before(band, i)
                if not (isinstance(r, int) and r == 0):
                    partial = band > 1 or (band == 1 and not isinstance(i, int))
                    tail = list(tail_b(r - 1, partial, B.before(band, i), l))
                    tail.pop(0)()
                blocks = B.bands[band]
                summed = 0
                for k, (_, _, in_sum) in enumerate(blocks):
                    if not in_sum:
                        continue
                    mask(l + summed, k % RING, summed % 4, landed(B, A.total, band, i, k))
                    if summed:
                        exponent(l + summed - 1, (summed - 1) % 4)
                    for _ in range(2 if summed == 0 else 1):
                        if tail:
                            tail.pop(0)()
                    summed += 1
                if summed:
                    exponent(l + summed - 1, (summed - 1) % 4)
                for step in tail:
                    step()

            def row_of_c(band, i, r):
                start = isinstance(r, int) and r == 0
                l = B.total_sums + C.sums_before(band, i)
                tail = list(tail_b(G - 1, True, B.total, l) if start else tail_c(r - 1, l))
                if start:
                    tail.pop(0)()
                for k in range(len(C.bands[band])):
                    mask(l + k, k % RING, k % 4, landed(C, A.total + B.total, band, i, k))
                    if k or not start:
                        exponent(l + k - 1, (k - 1) % 4)
                    if tail and (start or k != 1):
                        tail.pop(0)()
                assert not tail

            dve.memset(ones_b[:, :], 1.0).then_inc(consts_set, 1)
            dve.memset(ones_row[:, :], 1.0).then_inc(consts_set, 1)
            dve.memset(tiny_c[:, :], TINY).then_inc(consts_set, 1)
            dve.memset(minus2_c[:, :], -2.0).then_inc(consts_set, 1)
            each_row(dve, A, row_of_a, peeled=2)
            for step in tail_a(G - 1, True):
                step()
            each_row(dve, B, row_of_b, peeled=2)
            each_row(dve, C, row_of_c)
            exponent(B.total_sums + C.total_sums - 1, 3)
            for step in tail_c(G - 1, B.total_sums + C.total_sums):
                step()

        @block.scalar
        def _(act):
            def tanh_a(c):
                act.wait_ge(ta_pe, c * A_PE + 2)
                if not (isinstance(c, int) and c == 0):
                    act.wait_ge(kept_z1, c * 16)
                act.activation(tanh_t[:, :], pre_p[:, :], ACT.Tanh).then_inc(ta_act, 1)

            def root(dve_sem, dve_value, own, own_value):
                act.wait_ge(dve_sem, dve_value)
                act.activation(ln_var[:, :], var_eps[:, :], ACT.Ln).then_inc(own, 1)
                act.wait_ge(own, own_value + 1)
                act.activation(rstd0[:, :], ln_var[:, :], ACT.Exp, scale=-0.5).then_inc(own, 1)

            def tail_b(r):
                def tanh_b():
                    act.wait_ge(tb_pe, r * B_PE + 1)
                    if isinstance(r, int) and r == 0:
                        act.wait_ge(kept_z1, G * 16)
                    act.activation(tanh_t[:, :], pre_p[:, :], ACT.Tanh).then_inc(tb_act, 1)
                    act.preload_act_table_set("natural_log_exp_and_others")

                def root_b():
                    root(tb_dve, r * B_DVE + B_VAR, tb_act, r * B_ACT + 1)

                return [tanh_b, root_b]

            def tail_c(r):
                return [lambda: root(tc_dve, r * C_DVE + C_VAR, tc_act, r * C_ACT)]

            def inverse_square(l, buf):
                act.wait_ge(abs_done, l + 1)
                act.activation(logs[:, buf, :], logs[:, buf, :], ACT.Ln, bias=tiny_c[:, :]).then_inc(ln_done, 1)
                act.wait_ge(ln_done, l + 1)
                act.activation(logs[:, buf, :], logs[:, buf, :], ACT.Exp, scale=-2.0).then_inc(square_done, 1)

            def weight(l, buf):
                act.wait_ge(exponent_done, l + 1)
                if not (isinstance(l, int) and l < 2):
                    act.wait_ge(weight_read, l - 1)
                act.activation(weights[:, buf % 2, :], logs[:, buf, :], ACT.Exp, bias=minus2_c[:, :],
                               scale=4.0).then_inc(weight_done, 1)

            def row_of_b(band, i, r):
                tail = [] if isinstance(r, int) and r == 0 else tail_b(r - 1)
                l = B.sums_before(band, i)
                count = len(B.sums[band])
                if tail:
                    tail.pop(0)()
                for j in range(count):
                    inverse_square(l + j, j % 4)
                    if tail:
                        tail.pop(0)()
                    if j:
                        weight(l + j - 1, (j - 1) % 4)
                if count:
                    weight(l + count - 1, (count - 1) % 4)
                for step in tail:
                    step()

            def row_of_c(band, i, r):
                start = isinstance(r, int) and r == 0
                tail = tail_b(G - 1) if start else tail_c(r - 1)
                if not start:
                    act.preload_act_table_set("natural_log_exp_and_others")
                l = B.total_sums + C.sums_before(band, i)
                for j in range(len(C.bands[band])):
                    inverse_square(l + j, j % 4)
                    if j or not start:
                        weight(l + j - 1, (j - 1) % 4)
                    if tail and j in ((0, 1) if start else (2,)):
                        tail.pop(0)()
                assert not tail

            act.wait_ge(consts_set, 4)
            tanh_a(0)
            with act.Fori(1, G) as c:
                tanh_a(c)
            each_row(act, B, row_of_b, peeled=2)
            each_row(act, C, row_of_c)
            weight(B.total_sums + C.total_sums - 1, 3)
            for step in tail_c(G - 1):
                step()


def kernel(x, adj, L0_gnn_W_stack, L0_gnn_B_stack, L1_gnn_W, L1_gnn_B):
    import numpy as np
    import concourse.bacc as bacc
    from concourse.bass_utils import run_bass_kernel_spmd

    x, adj = np.asarray(x), np.asarray(adj)
    n = adj.shape[0]
    groups = n // ROW
    blocks = np.ascontiguousarray(adj.reshape(groups, ROW, groups, T, P).transpose(0, 2, 4, 3, 1))
    arrays = {
        "x": np.ascontiguousarray(x),
        "x_t": np.ascontiguousarray(x.T),
        "adj": blocks,
        "w_stack": np.ascontiguousarray(L0_gnn_W_stack),
        "b_stack": np.ascontiguousarray(L0_gnn_B_stack),
        "w_msg": np.ascontiguousarray(L1_gnn_W),
        "bias_msg": np.ascontiguousarray(np.asarray(L1_gnn_B).reshape(1, -1)),
    }
    nc = bacc.Bacc("TRN2", target_bir_lowering=False, num_devices=1)
    args = [nc.dram_tensor(k, v.shape, mybir.dt.from_np(v.dtype), kind="ExternalInput").ap()
            for k, v in arrays.items()]
    out = nc.dram_tensor("out", x.shape, mybir.dt.from_np(x.dtype), kind="ExternalOutput").ap()
    graph_kernel(nc, *args, out)
    return run_bass_kernel_spmd(nc, [arrays], core_ids=[0]).results[0]["out"]
```

```python
from collections import namedtuple
from contextlib import ExitStack

import concourse.bass as bass
from concourse import mybir

P = 128
D = 128
ROW = 512
T = ROW // P
RING = 4
BAND = 4
EPS = 1e-5
LAG = 3
TINY = 1e-15


Block = namedtuple("Block", "g layer2 weighed summed kept")


class Pass:

    def __init__(self, bands):
        self.bands = bands

    def before(self, band, i, k=0, which=lambda k, b: True):
        rows = [[which(place, b) for place, b in enumerate(blocks)] for blocks in self.bands]
        n = BAND * sum(map(sum, rows[:band])) + sum(rows[band][:k])
        return n + i * sum(rows[band]) if sum(rows[band]) else n

    def total(self, which=lambda k, b: True):
        return BAND * sum(which(k, b) for blocks in self.bands for k, b in enumerate(blocks))


def weighed(k, b):
    return b.weighed


def summed(k, b):
    return b.weighed and b.summed


def spread(few, many):
    step, many = len(many) // 4 + 1, iter(many)
    return [few[k // step] if k % step == 0 else next(many) for k in range(4 * step)]


def passes(groups):
    lows = range(0, groups, BAND)
    up = [[Block(g, g < lo, False, False, None) for g in [*range(lo, groups), *range(lo)]] for lo in lows]
    down = [spread([Block(g, True, True, False, g - lo) for g in range(lo + BAND - 1, lo - 1, -1)],
                   [Block(g, True, True, True, None) for g in range(groups - 1, lo + BAND - 1, -1)])
            for lo in reversed(lows)]
    rest = [spread([Block(g, False, False, True, g - lo) for g in range(lo + BAND - 1, lo - 1, -1)],
                   [Block(g, False, True, True, None) for g in range(lo - 1, -1, -1)])
            for lo in reversed(lows)]
    return Pass(up), Pass(down), Pass(rest)


def each_row(engine, table, row, peeled=None):
    for band in range(len(table.bands)):
        first = 0
        if peeled is None or band < peeled:
            row(band, 0, band * BAND)
            first = 1
        with engine.Fori(first, BAND) as i:
            row(band, i, i + band * BAND)


def earlier(table, band, i, k, d):
    if k >= d:
        return band, i, k - d
    if not isinstance(i, int):
        return band, i - 1, len(table.bands[band]) + k - d
    if band:
        return band - 1, BAND - 1, len(table.bands[band - 1]) + k - d
    return None


B_PLACES = {
    4: dict(dve=(0, 2, 2, 3, 3, 3), pe=(0, 1, 3, 3), act=(0, 3)),
    8: dict(dve=(0, 3, 3, 4, 6, 7), pe=(1, 2, 5, 6), act=(1, 4)),
    12: dict(dve=(0, 3, 4, 6, 8, 9), pe=(1, 3, 7, 8), act=(2, 5)),
    16: dict(dve=(0, 3, 4, 6, 8, 9), pe=(1, 3, 7, 8), act=(2, 5)),
}
C_PLACES = {
    4: dict(dve=(3, 3, 3), pe=(2,), act=(3,)),
    8: dict(dve=(3, 5, 7), pe=(4,), act=(6,)),
    12: dict(dve=(4, 6, 8), pe=(5,), act=(7,)),
    16: dict(dve=(4, 6, 8), pe=(5,), act=(7,)),
}


class Steps:

    def __init__(self, engine, sem, base):
        self.engine, self.sem, self.base, self.n = engine, sem, base, 0

    def did(self, instruction):
        self.n += 1
        return instruction.then_inc(self.sem, 1)

    def settle(self):
        self.engine.wait_ge(self.sem, self.base + self.n)


def graph_kernel(nc: bass.Bass, x, x_t, adj, w_stack, b_stack, w_msg, bias_msg, out):
    dt = mybir.dt
    f32, bf16, u32 = dt.float32, dt.bfloat16, dt.uint32
    ALU, ACT = mybir.AluOpType, mybir.ActivationFunctionType

    G = x.shape[0] // ROW
    A, B, C = passes(G)
    ALL_A, ALL_B = A.total(), B.total()
    SUMS_B = B.total(summed)
    WEIGHED = ALL_B + C.total(weighed)
    LAST = G // BAND - 1

    inv_deg_d = nc.dram_tensor("inv_deg_d", (G, P, ROW), f32, kind="Internal").ap()
    agg_d = nc.dram_tensor("agg_d", (G, P, ROW), f32, kind="Internal").ap()
    z1t_d = nc.dram_tensor("z1t_d", (G, P, ROW), f32, kind="Internal").ap()
    sum_d = nc.dram_tensor("sum_d", (G, P, ROW), f32, kind="Internal").ap()
    weights_d = nc.dram_tensor("weights_d", (G, BAND, P, T * ROW), f32, kind="Internal").ap()
    x1_d = nc.dram_tensor("x1_d", (G, P, T, D), f32, kind="Internal").ap()

    x_rows = x.rearrange("(c t p) d -> c p t d", t=T, p=P)
    out_rows = out.rearrange("(c t p) d -> c p t d", t=T, p=P)
    x_tiles = x.rearrange("(g p) d -> p g d", p=P)
    x_t_rows = x_t.rearrange("d (c n) -> c d n", n=ROW)

    ctx = ExitStack()
    with ctx:
        def sb(name, shape, dtype=f32):
            return ctx.enter_context(nc.sbuf_tensor(name, shape, dtype))

        def pb(name, shape):
            return ctx.enter_context(nc.psum_tensor(name, shape, f32))

        def sem(name):
            return ctx.enter_context(nc.semaphore(name))

        x_msg = sb("x_msg", [P, G * T, D])
        z1_nat = sb("z1_nat", [P, G * T, D])
        ring = sb("ring", [P, RING, T, ROW])
        masked = sb("masked", [P, 2, T * ROW])
        logs = sb("logs", [P, 4, T * ROW])
        weights = sb("weights", [P, 2, T * ROW])
        nonzero = sb("nonzero", [P, 2, T * ROW], bf16)
        ones_b = sb("ones_b", [P, P], bf16)
        ones_row = sb("ones_row", [1, P])
        ident = sb("ident", [P, P])
        w0, w1, b0, b1, wm = (sb(n, [P, D]) for n in ("w0", "w1", "b0", "b1", "wm"))
        bias_row = sb("bias_row", [1, D])
        tiny_c = sb("tiny_c", [P, 1])
        minus2_c = sb("minus2_c", [P, 1])
        inv_t = sb("inv_t", [P, ROW])
        deg_t = sb("deg_t", [P, ROW])
        part_t = sb("part_t", [P, ROW])
        agg_t = sb("agg_t", [P, ROW])
        side_t = sb("side_t", [P, ROW])
        tanh_t = sb("tanh_t", [P, ROW])
        sum_t = sb("sum_t", [P, ROW])
        res_t = sb("res_t", [P, T, D])
        pre_t = sb("pre_t", [P, T, D])
        norm_t = sb("norm_t", [P, T, D])
        x1t_t = sb("x1t_t", [P, T, P])
        stats = sb("stats", [P, T, 6])
        mean_var = sb("mean_var", [P, T, 2])
        var_eps, ln_var, rstd0, newton, rstd = (
            sb(n, [P, T]) for n in ("var_eps", "ln_var", "rstd0", "newton", "rstd"))

        acc_p = pb("acc_p", [P, 2, ROW])
        acc_q = pb("acc_q", [P, 2, ROW])
        deg_p = pb("deg_p", [P, ROW])
        pre_p = pb("pre_p", [P, ROW])
        turn_p = pb("turn_p", [P, T, P])
        msg_p = pb("msg_p", [P, T, D])

        consts_in, x_in, consts_set, ident_set = map(sem, ("consts_in", "x_in", "consts_set", "ident_set"))
        adj_in = [sem(f"adj_in{k}") for k in range(RING)]
        adj_pe = sem("adj_pe")
        adj_dve = sem("adj_dve")
        abs_done, ln_done, square_done = map(sem, ("abs_done", "ln_done", "square_done"))
        exponent_done, weight_done = map(sem, ("exponent_done", "weight_done"))
        weight_read = sem("weight_read")
        kept_weights = [sem(f"kept_weights{k}") for k in range(4)]
        ta_pe, ta_dve, ta_act = map(sem, ("ta_pe", "ta_dve", "ta_act"))
        tb_pe, tb_dve, tb_act = map(sem, ("tb_pe", "tb_dve", "tb_act"))
        tc_pe, tc_dve, tc_act = map(sem, ("tc_pe", "tc_dve", "tc_act"))
        side_a, side_b, side_c = map(sem, ("side_a", "side_b", "side_c"))
        kept_inv, kept_agg, kept_z1, kept_sum, kept_x1, kept_out = map(
            sem, ("kept_inv", "kept_agg", "kept_z1", "kept_sum", "kept_x1", "kept_out"))

        A_PE, A_DVE, A_ACT = 3, 5, 1
        A_AGG, A_Z1 = 4, 5
        NORM = 1 + T + T + 1
        FINISH = 3 + T
        B_PE, B_ACT = 4, 3
        B_AGG, B_SUM, B_VAR = 2, 3, 3 + NORM
        B_X1 = B_VAR + 1 + FINISH
        B_X1T, B_MSG = B_X1 + 1, B_X1 + 2
        B_DVE = B_MSG
        C_PE, C_ACT = 1, 2
        C_SUM, C_VAR = 1, 1 + NORM
        C_OUT = C_DVE = C_VAR + 1 + FINISH

        def apart(engine):
            engine.sem_inc(passed[engine], 1)

        def landed(table, loads_before, band, i, k):
            in_slot = loads_before // RING + table.before(band, 0) // RING + k // RING + 1
            return 16 * (i * (len(table.bands[band]) // RING) + in_slot)

        def keeps(slot):
            return lambda k, b: b.kept is not None and k % 4 == slot

        passed = {nc.sync: sem("passed_sp"), nc.gpsimd: sem("passed_pool"), nc.vector: sem("passed_dve"),
                  nc.scalar: sem("passed_act")}

        block = ctx.enter_context(nc.Block())

        @block.sync
        def _(sp):
            quarter = G * T // 4

            def load(k, c, g):
                sp.dma_start(ring[:, k % RING, :, :], adj[c, g]).then_inc(adj_in[k % RING], 16)

            for tile, src in ((w0, w_stack[0]), (b0, b_stack[0]), (w1, w_stack[1]),
                              (b1, b_stack[1]), (wm, w_msg), (bias_row, bias_msg)):
                sp.dma_start(tile[:, :], src).then_inc(consts_in, 16)

            def load_row_a(band, i, r):
                for k, b in enumerate(A.bands[band]):
                    n = A.before(band, i) + k
                    if not (isinstance(n, int) and n < RING):
                        sp.wait_ge(adj_pe, n - RING + 1)
                        sp.wait_ge(adj_dve, n - RING + 1)
                    apart(sp)
                    load(k, r, b.g)
                    if isinstance(n, int) and n < 4:
                        tiles = slice(n * quarter, (n + 1) * quarter)
                        sp.dma_start(x_msg[:, tiles, :], x_tiles[:, tiles, :]).then_inc(x_in, 16)

            def load_row_b(band, i, r):
                for k, b in enumerate(B.bands[band]):
                    l = ALL_A + B.before(band, i, k)
                    sp.wait_ge(adj_pe, l - RING + 1)
                    sp.wait_ge(adj_dve, l - RING + 1)
                    apart(sp)
                    load(k, G - 1 - r, b.g)

            def load_row_c(band, i, r):
                if isinstance(r, int) and r == 0:
                    for k, kept in enumerate(kept_weights):
                        sp.wait_ge(kept, 16 * B.before(0, 1, 0, keeps(k)))
                elif band == 0:
                    for k, kept in enumerate(kept_weights):
                        sp.wait_ge(kept, 16 * B.total(keeps(k)))
                for k, b in enumerate(C.bands[band]):
                    last = earlier(C, band, i, k, RING)
                    if last is None:
                        sp.wait_ge(adj_pe, ALL_A + ALL_B - RING + 1 + k)
                        sp.wait_ge(adj_dve, ALL_A + ALL_B - RING + 1 + k)
                    elif C.bands[last[0]][last[2]].weighed:
                        sp.wait_ge(adj_dve, ALL_A + ALL_B + C.before(*last, weighed) + 1)
                    else:
                        sp.wait_ge(adj_pe, ALL_A + ALL_B + C.before(*last, lambda k, b: not b.weighed) + 1)
                    apart(sp)
                    if b.weighed:
                        load(k, G - 1 - r, b.g)
                    else:
                        sp.dma_start(ring[:, k % RING, :, :].rearrange("p t n -> p (t n)"),
                                     weights_d[G - 1 - r, b.kept]).then_inc(adj_in[k % RING], 16)

            each_row(sp, A, load_row_a, peeled=1)
            each_row(sp, B, load_row_b, peeled=0)
            each_row(sp, C, load_row_c)

        @block.gpsimd
        def _(pool):
            pool.memset(ident[:, :], 0.0).then_inc(ident_set, 1)
            pool.wait_ge(ident_set, 1)
            pool.affine_select(out=ident[:, :], in_=ident[:, :], compare_op=ALU.not_equal, fill=1.0,
                               base=0, pattern=[[-1, P]], channel_multiplier=1).then_inc(ident_set, 1)

            def side_row_a(c):
                if not (isinstance(c, int) and c == 0):
                    pool.wait_ge(ta_pe, c * A_PE)
                apart(pool)
                pool.dma_start(side_t[:, :], x_t_rows[c]).then_inc(side_a, 16)
                pool.wait_ge(ta_dve, c * A_DVE + A_AGG)
                apart(pool)
                pool.dma_start(inv_deg_d[c], inv_t[:, :]).then_inc(kept_inv, 16)
                pool.dma_start(agg_d[c], part_t[:, :]).then_inc(kept_agg, 16)
                pool.wait_ge(ta_act, c * A_ACT + 1)
                apart(pool)
                pool.dma_start(z1t_d[c], tanh_t[:, :]).then_inc(kept_z1, 16)

            def side_row_b(r):
                c = G - 1 - r
                if isinstance(r, int) and r == 0:
                    pool.wait_ge(ta_dve, G * A_DVE)
                    pool.wait_ge(kept_inv, 16 * G)
                    pool.wait_ge(kept_agg, 16 * G)
                    pool.wait_ge(kept_z1, 16 * G)
                else:
                    pool.wait_ge(tb_dve, r * B_DVE)
                    pool.wait_ge(kept_x1, r * 16)
                apart(pool)
                pool.dma_start(inv_t[:, :], inv_deg_d[c]).then_inc(side_b, 16)
                pool.dma_start(part_t[:, :], agg_d[c]).then_inc(side_b, 16)
                pool.dma_start(side_t[:, :], z1t_d[c]).then_inc(side_b, 16)
                pool.dma_start(res_t[:, :, :], x_rows[c]).then_inc(side_b, 16)
                pool.wait_ge(tb_dve, r * B_DVE + B_SUM)
                apart(pool)
                pool.dma_start(sum_d[c], sum_t[:, :]).then_inc(kept_sum, 16)
                pool.wait_ge(tb_dve, r * B_DVE + B_X1)
                apart(pool)
                pool.dma_start(x1_d[c], norm_t[:, :, :]).then_inc(kept_x1, 16)

            def side_row_c(r):
                c = G - 1 - r
                if isinstance(r, int) and r == 0:
                    pool.wait_ge(tb_dve, G * B_DVE)
                    pool.wait_ge(kept_sum, 16 * G)
                    pool.wait_ge(kept_x1, 16 * G)
                else:
                    pool.wait_ge(tc_dve, r * C_DVE)
                apart(pool)
                pool.dma_start(part_t[:, :], sum_d[c]).then_inc(side_c, 16)
                pool.dma_start(res_t[:, :, :], x1_d[c]).then_inc(side_c, 16)
                pool.wait_ge(tc_dve, r * C_DVE + C_OUT)
                apart(pool)
                pool.dma_start(out_rows[c], norm_t[:, :, :]).then_inc(kept_out, 16)

            for side_row in (side_row_a, side_row_b, side_row_c):
                side_row(0)
                with pool.Fori(1, G) as r:
                    side_row(r)
            pool.wait_ge(kept_out, 16 * G)

        @block.tensor
        def _(pe):
            def product(acc, stationary, moving, first, last):
                for t in range(T):
                    mm = pe.matmul(acc, stationary[:, t, :], moving[:, t, :],
                                   start=first and t == 0, stop=last and t == T - 1)
                return mm

            def tiles(z, g):
                return z[:, g * T:(g + 1) * T, :]

            def turn(steps, src):
                for t in range(T):
                    mm = pe.transpose(turn_p[:, t, :], src[:, t, :], ident[:, :])
                steps.did(mm)

            def tail_a(c):
                steps = Steps(pe, ta_pe, c * A_PE)

                def degree():
                    pe.wait_ge(adj_dve, (c + 1) * G)
                    for t in range(T):
                        mm = pe.matmul(deg_p[:, :], ones_b[:, :], nonzero[:, c % 2, t * ROW:(t + 1) * ROW],
                                       start=t == 0, stop=t == T - 1)
                    steps.did(mm)

                def layer():
                    pe.wait_ge(ta_dve, c * A_DVE + A_AGG)
                    pe.wait_ge(side_a, (c + 1) * 16)
                    pe.matmul(pre_p[:, :], w0[:, :], agg_t[:, :], start=True, stop=False)
                    steps.did(pe.matmul(pre_p[:, :], b0[:, :], side_t[:, :], start=False, stop=True))

                def turn_z1():
                    pe.wait_ge(ta_act, c * A_ACT + 1)
                    turn(steps, tanh_t[:, :].rearrange("d (t p) -> d t p", p=P))

                return degree, layer, turn_z1

            def tail_b(r):
                steps = Steps(pe, tb_pe, r * B_PE)

                def layer():
                    pe.wait_ge(tb_dve, r * B_DVE + B_AGG)
                    pe.wait_ge(side_b, (r + 1) * 64)
                    pe.matmul(pre_p[:, :], w1[:, :], agg_t[:, :], start=True, stop=False)
                    steps.did(pe.matmul(pre_p[:, :], b1[:, :], side_t[:, :], start=False, stop=True))

                def turn_z2():
                    pe.wait_ge(tb_act, r * B_ACT + 1)
                    turn(steps, tanh_t[:, :].rearrange("d (t p) -> d t p", p=P))

                def turn_x1():
                    pe.wait_ge(tb_dve, r * B_DVE + B_X1)
                    turn(steps, norm_t)

                def messages():
                    pe.wait_ge(tb_dve, r * B_DVE + B_X1T)
                    for t in range(T):
                        pe.matmul(msg_p[:, t, :], x1t_t[:, t, :], wm[:, :], start=True, stop=False)
                        mm = pe.matmul(msg_p[:, t, :], ones_row[:, :], bias_row[:, :], start=False, stop=True)
                    steps.did(mm)

                return layer, turn_z2, turn_x1, messages

            def tail_c(r):
                steps = Steps(pe, tc_pe, r * C_PE)

                def turn_sum():
                    pe.wait_ge(tc_dve, r * C_DVE + C_SUM)
                    turn(steps, sum_t[:, :].rearrange("d (t p) -> d t p", p=P))

                return (turn_sum,)

            def row_of_a(band, i, r):
                blocks = A.bands[band]
                degree, layer, turn_z1 = tail_a(r - 1)
                tail = not (isinstance(r, int) and r == 0)
                if tail:
                    degree()
                for k, b in enumerate(blocks):
                    if isinstance(r, int) and r == 0 and k % (G // 4) == 0:
                        pe.wait_ge(x_in, 64)
                    pe.wait_ge(adj_in[k % RING], landed(A, 0, band, i, k))
                    mm = product(acc_p[:, r % 2, :], tiles(x_msg, b.g), ring[:, k % RING], k == 0, k == G - 1)
                    if b.layer2:
                        pe.wait_ge(ta_dve, (b.g + 1) * A_DVE)
                        mm = product(acc_q[:, r % 2, :], tiles(z1_nat, b.g), ring[:, k % RING],
                                     b.g == 0, k == G - 1)
                    mm.then_inc(adj_pe, 1)
                    if tail and k == 1:
                        layer()
                    if tail and k == 2:
                        turn_z1()

            def sum_messages(table, band, i, k):
                blocks = table.bands[band]
                b, r = blocks[k], band * BAND + i
                if not (b.weighed and b.summed):
                    return
                if table is B:
                    acc, ordinal, l = acc_q, sum(x.summed for x in blocks[:k]), B.before(band, i, k)
                    first = ordinal == 0
                else:
                    acc, ordinal, l = acc_p, sum(x.weighed for x in blocks[:k]), ALL_B + C.before(band, i, k, weighed)
                    first = False
                pe.wait_ge(tb_dve, (G - b.g) * B_DVE)
                pe.wait_ge(weight_done, l + 1)
                mm = product(acc[:, r % 2, :], tiles(x_msg, b.g),
                             weights[:, ordinal % 2, :].rearrange("p (t n) -> p t n", t=T),
                             first, k == len(blocks) - 1)
                mm.then_inc(weight_read, 1)

            def row_of_b(band, i, r):
                blocks = B.bands[band]
                tail = () if isinstance(r, int) and r == 0 else tail_b(r - 1)
                for k, b in enumerate(blocks):
                    pe.wait_ge(adj_in[k % RING], landed(B, ALL_A, band, i, k))
                    pe.wait_ge(ta_dve, (b.g + 1) * A_DVE)
                    mm = product(acc_p[:, r % 2, :], tiles(z1_nat, b.g), ring[:, k % RING],
                                 k == 0, k == len(blocks) - 1)
                    mm.then_inc(adj_pe, 1)
                    last = earlier(B, band, i, k, LAG)
                    if last:
                        sum_messages(B, *last)
                    for step, place in zip(tail, B_PLACES[len(blocks)]["pe"]):
                        if place == k:
                            step()

            def row_of_c(band, i, r):
                blocks = C.bands[band]
                start = isinstance(r, int) and r == 0
                tail = tail_b(G - 1) if start else tail_c(r - 1)
                for k, b in enumerate(blocks):
                    if not b.weighed:
                        pe.wait_ge(adj_in[k % RING], landed(C, ALL_A + ALL_B, band, i, k))
                        if start:
                            pe.wait_ge(tb_dve, (G - b.g) * B_DVE)
                        mm = product(acc_p[:, r % 2, :], tiles(x_msg, b.g), ring[:, k % RING],
                                     k == 0, k == len(blocks) - 1)
                        mm.then_inc(adj_pe, 1)
                    last = earlier(C, band, i, k, LAG)
                    if last:
                        sum_messages(C, *last)
                    else:
                        sum_messages(B, LAST, BAND - 1, G - LAG + k)
                    for step, place in zip(tail, (B_PLACES if start else C_PLACES)[len(blocks)]["pe"]):
                        if place == k:
                            step()

            pe.wait_ge(consts_in, 6 * 16)
            pe.wait_ge(consts_set, 4)
            pe.wait_ge(ident_set, 2)
            each_row(pe, A, row_of_a, peeled=1)
            for step in tail_a(G - 1):
                step()
            each_row(pe, B, row_of_b)
            each_row(pe, C, row_of_c)
            for step in tail_c(G - 1):
                step()

        @block.vector
        def _(dve):
            def norm_stats(steps, pe_sem, pe_value, side_sem, side_value):
                dve.wait_ge(pe_sem, pe_value)
                dve.wait_ge(side_sem, side_value)
                steps.did(dve.tensor_tensor(out=pre_t[:, :, :], in0=turn_p[:, :, :], in1=res_t[:, :, :], op=ALU.add))
                steps.settle()
                for t in range(T):
                    steps.did(dve.bn_stats(out=stats[:, t, :], in_=pre_t[:, t, :]))
                steps.settle()
                apart(dve)
                for t in range(T):
                    steps.did(dve.bn_aggr(out=mean_var[:, t, :], in_=stats[:, t, :]))
                steps.settle()
                steps.did(dve.tensor_scalar(var_eps[:, :], mean_var[:, :, 1], EPS, None, ALU.add))

            def norm_finish(steps, act_sem, act_value, kept, kept_value):
                dve.wait_ge(act_sem, act_value)
                steps.did(dve.tensor_tensor(out=newton[:, :], in0=rstd0[:, :], in1=rstd0[:, :], op=ALU.mult))
                steps.settle()
                steps.did(dve.tensor_tensor(out=newton[:, :], in0=newton[:, :], in1=var_eps[:, :], op=ALU.mult))
                steps.settle()
                steps.did(dve.tensor_scalar(newton[:, :], newton[:, :], -0.5, 1.5, ALU.mult, ALU.add))
                steps.settle()
                steps.did(dve.tensor_tensor(out=rstd[:, :], in0=newton[:, :], in1=rstd0[:, :], op=ALU.mult))
                steps.settle()
                if kept_value is not None:
                    dve.wait_ge(kept, kept_value)
                for t in range(T):
                    steps.did(dve.tensor_scalar(norm_t[:, t, :], pre_t[:, t, :], mean_var[:, t, 0:1],
                                                rstd[:, t:t + 1], ALU.subtract, ALU.mult))

            def tail_a(c, partial):
                steps = Steps(dve, ta_dve, c * A_DVE)
                first = isinstance(c, int) and c == 0

                def aggregate():
                    dve.wait_ge(ta_pe, c * A_PE + 1)
                    dve.wait_ge(adj_pe, (c + 1) * G)
                    if not first:
                        dve.wait_ge(kept_inv, c * 16)
                        dve.wait_ge(kept_agg, c * 16)
                    steps.did(dve.tensor_scalar(deg_t[:, :], deg_p[:, :], 1.0, None, ALU.max))
                    if partial:
                        steps.did(dve.tensor_copy(part_t[:, :], acc_q[:, c % 2, :]))
                    else:
                        steps.did(dve.memset(part_t[:, :], 0.0))
                    steps.settle()
                    steps.did(dve.reciprocal(inv_t[:, :], deg_t[:, :]))
                    steps.settle()
                    steps.did(dve.tensor_tensor(out=agg_t[:, :], in0=acc_p[:, c % 2, :], in1=inv_t[:, :], op=ALU.mult))

                def keep_z1():
                    dve.wait_ge(ta_pe, c * A_PE + 3)
                    apart(dve)
                    steps.did(dve.tensor_copy(z1_nat[:, bass.ds(c * T, T), :], turn_p[:, :, :]))

                return aggregate, keep_z1

            def tail_b(r, partial, blocks, sums):
                steps = Steps(dve, tb_dve, r * B_DVE)
                first = isinstance(r, int) and r == 0

                def aggregate():
                    dve.wait_ge(adj_pe, ALL_A + blocks)
                    dve.wait_ge(side_b, (r + 1) * 64)
                    steps.did(dve.tensor_tensor(out=agg_t[:, :], in0=acc_p[:, r % 2, :], in1=part_t[:, :], op=ALU.add))
                    steps.settle()
                    steps.did(dve.tensor_tensor(out=agg_t[:, :], in0=agg_t[:, :], in1=inv_t[:, :], op=ALU.mult))

                def partial_sum():
                    if not first:
                        dve.wait_ge(kept_sum, r * 16)
                    if partial:
                        dve.wait_ge(weight_read, sums)
                        steps.did(dve.tensor_copy(sum_t[:, :], acc_q[:, r % 2, :]))
                    else:
                        steps.did(dve.memset(sum_t[:, :], 0.0))

                def norm_in():
                    norm_stats(steps, tb_pe, r * B_PE + 2, side_b, (r + 1) * 64)

                def norm_out():
                    norm_finish(steps, tb_act, r * B_ACT + 3, kept_x1, None if first else r * 16)

                def keep_x1t():
                    dve.wait_ge(tb_pe, r * B_PE + 3)
                    steps.did(dve.tensor_copy(x1t_t[:, :, :], turn_p[:, :, :]))

                def keep_messages():
                    dve.wait_ge(tb_pe, r * B_PE + 4)
                    apart(dve)
                    steps.did(dve.tensor_copy(x_msg[:, bass.ds((G - 1 - r) * T, T), :], msg_p[:, :, :]))
                    assert steps.n == B_DVE

                return aggregate, partial_sum, norm_in, norm_out, keep_x1t, keep_messages

            def tail_c(r, sums, kept):
                steps = Steps(dve, tc_dve, r * C_DVE)
                first = isinstance(r, int) and r == 0

                def whole_sum():
                    dve.wait_ge(weight_read, sums)
                    dve.wait_ge(adj_pe, kept)
                    dve.wait_ge(side_c, (r + 1) * 32)
                    if first:
                        dve.wait_ge(kept_sum, G * 16)
                    steps.did(dve.tensor_tensor(out=sum_t[:, :], in0=acc_p[:, r % 2, :], in1=part_t[:, :], op=ALU.add))

                def norm_in():
                    norm_stats(steps, tc_pe, r * C_PE + 1, side_c, (r + 1) * 32)

                def norm_out():
                    norm_finish(steps, tc_act, r * C_ACT + 2, kept_x1 if first else kept_out,
                                G * 16 if first else r * 16)
                    assert steps.n == C_DVE

                return whole_sum, norm_in, norm_out

            def mask(l, slot, buf, in_value, kept_value=None):
                dve.wait_ge(adj_in[slot], in_value)
                if not (isinstance(l, int) and l < 2):
                    dve.wait_ge(exponent_done, l - 1)
                r = ring[:, slot].rearrange("p t n -> p (t n)")
                dve.scalar_tensor_tensor(out=masked[:, buf % 2, :], in0=r, scalar=1.0, in1=r,
                                         op0=ALU.is_lt, op1=ALU.mult).then_inc(adj_dve, 1)
                dve.wait_ge(adj_dve, ALL_A + l + 1)
                if kept_value is not None:
                    dve.wait_ge(kept_weights[buf], kept_value)
                elif not (isinstance(l, int) and l < 4):
                    dve.wait_ge(weight_done, l - 3)
                dve.tensor_scalar(logs[:, buf, :].bitcast(u32), masked[:, buf % 2, :].bitcast(u32), 0x7FFFFFFF,
                                  None, ALU.bitwise_and).then_inc(abs_done, 1)

            def exponent(l, buf):
                dve.wait_ge(square_done, l + 1)
                dve.scalar_tensor_tensor(out=logs[:, buf, :], in0=masked[:, buf % 2, :], scalar=-0.5,
                                         in1=logs[:, buf, :], op0=ALU.add, op1=ALU.mult
                                         ).then_inc(exponent_done, 1)

            def row_of_a(band, i, r):
                tail = not (isinstance(r, int) and r == 0)
                aggregate, keep_z1 = tail_a(r - 1, band > 0 and not (band == 1 and isinstance(i, int)))
                for k in range(G):
                    n = A.before(band, i) + k
                    dve.wait_ge(adj_in[k % RING], landed(A, 0, band, i, k))
                    seen = ring[:, k % RING].rearrange("p t n -> p (t n)")
                    counts = nonzero[:, r % 2, :]
                    if k == 0:
                        dve.tensor_scalar(counts, seen, 0.0, None, ALU.not_equal).then_inc(adj_dve, 1)
                    else:
                        dve.wait_ge(adj_dve, n)
                        dve.scalar_tensor_tensor(out=counts, in0=seen, scalar=0.0, in1=counts,
                                                 op0=ALU.not_equal, op1=ALU.add).then_inc(adj_dve, 1)
                    if tail and k == 1:
                        aggregate()
                    if tail and k == 3:
                        keep_z1()

            def row_of_b(band, i, r):
                blocks = B.bands[band]
                tail = ()
                if not (isinstance(r, int) and r == 0):
                    before = earlier(B, band, i, 0, 1)
                    tail = tail_b(r - 1, before[0] > 0, B.before(band, i), B.before(band, i, 0, summed))
                for k in range(len(blocks)):
                    l = B.before(band, i, k)
                    last = earlier(B, band, i, k, 4)
                    kept = last is not None and B.bands[last[0]][last[2]].kept is not None
                    mask(l, k % RING, k % 4, landed(B, ALL_A, band, i, k),
                         16 * (B.before(*last, keeps(k % 4)) + 1) if kept else None)
                    if not (isinstance(l, int) and l == 0):
                        exponent(l - 1, (k - 1) % 4)
                    for step, place in zip(tail, B_PLACES[len(blocks)]["dve"]):
                        if place == k:
                            step()

            def row_of_c(band, i, r):
                blocks = C.bands[band]
                start = isinstance(r, int) and r == 0
                if start:
                    tail, places = tail_b(G - 1, True, ALL_B, SUMS_B), B_PLACES[G]["dve"]
                else:
                    tail = tail_c(r - 1, SUMS_B + C.before(band, i, 0, weighed),
                                  ALL_A + ALL_B + r * BAND)
                    places = C_PLACES[len(blocks)]["dve"]
                for k, b in enumerate(blocks):
                    l = ALL_B + C.before(band, i, k, weighed)
                    buf = sum(x.weighed for x in blocks[:k]) % 4
                    if b.weighed:
                        kept = isinstance(l, int) and l == ALL_B + buf and B.bands[LAST][G - 4 + buf].kept is not None
                        mask(l, k % RING, buf, landed(C, ALL_A + ALL_B, band, i, k),
                             16 * B.total(keeps(buf)) if kept else None)
                    if b.weighed or (band == LAST and isinstance(i, int) and k == 0):
                        exponent(l - 1, (buf - 1) % 4)
                    for step, place in zip(tail, places):
                        if place == k:
                            step()

            dve.memset(ones_b[:, :], 1.0).then_inc(consts_set, 1)
            dve.memset(ones_row[:, :], 1.0).then_inc(consts_set, 1)
            dve.memset(tiny_c[:, :], TINY).then_inc(consts_set, 1)
            dve.memset(minus2_c[:, :], -2.0).then_inc(consts_set, 1)
            each_row(dve, A, row_of_a, peeled=2)
            for step in tail_a(G - 1, True):
                step()
            each_row(dve, B, row_of_b)
            each_row(dve, C, row_of_c)
            for step in tail_c(G - 1, SUMS_B + C.total(weighed), ALL_A + ALL_B + G * BAND):
                step()

        @block.scalar
        def _(act):
            def tanh_a(c):
                act.wait_ge(ta_pe, c * A_PE + 2)
                if not (isinstance(c, int) and c == 0):
                    act.wait_ge(kept_z1, c * 16)
                act.activation(tanh_t[:, :], pre_p[:, :], ACT.Tanh).then_inc(ta_act, 1)

            def root(dve_sem, dve_value, own, own_value):
                act.wait_ge(dve_sem, dve_value)
                act.activation(ln_var[:, :], var_eps[:, :], ACT.Ln).then_inc(own, 1)
                act.wait_ge(own, own_value + 1)
                act.activation(rstd0[:, :], ln_var[:, :], ACT.Exp, scale=-0.5).then_inc(own, 1)

            def tail_b(r):
                def tanh_b():
                    act.wait_ge(tb_pe, r * B_PE + 1)
                    if isinstance(r, int) and r == 0:
                        act.wait_ge(kept_z1, G * 16)
                    act.activation(tanh_t[:, :], pre_p[:, :], ACT.Tanh).then_inc(tb_act, 1)
                    act.preload_act_table_set("natural_log_exp_and_others")

                def root_b():
                    root(tb_dve, r * B_DVE + B_VAR, tb_act, r * B_ACT + 1)

                return [tanh_b, root_b]

            def tail_c(r):
                return [lambda: root(tc_dve, r * C_DVE + C_VAR, tc_act, r * C_ACT)]

            def inverse_square(l, buf):
                act.wait_ge(abs_done, l + 1)
                act.activation(logs[:, buf, :], logs[:, buf, :], ACT.Ln, bias=tiny_c[:, :]).then_inc(ln_done, 1)
                act.wait_ge(ln_done, l + 1)
                act.activation(logs[:, buf, :], logs[:, buf, :], ACT.Exp, scale=-2.0).then_inc(square_done, 1)

            def weight(table, band, i, k):
                blocks = table.bands[band]
                b = blocks[k]
                if table is B:
                    l, s, buf = B.before(band, i, k), B.before(band, i, k, summed), k % 4
                else:
                    l = ALL_B + C.before(band, i, k, weighed)
                    s, buf = SUMS_B + l - ALL_B, sum(x.weighed for x in blocks[:k]) % 4
                act.wait_ge(exponent_done, l + 1)
                if b.kept is None:
                    if not (isinstance(s, int) and s < 2):
                        act.wait_ge(weight_read, s - 1)
                    half = sum(x.weighed and x.summed for x in blocks[:k]) % 2
                    act.activation(weights[:, half, :], logs[:, buf, :], ACT.Exp, bias=minus2_c[:, :],
                                   scale=4.0).then_inc(weight_done, 1)
                else:
                    act.activation(logs[:, buf, :], logs[:, buf, :], ACT.Exp, bias=minus2_c[:, :],
                                   scale=4.0).then_inc(weight_done, 1)
                    act.wait_ge(weight_done, l + 1)
                    apart(act)
                    act.dma_start(weights_d[G - 1 - (band * BAND + i), b.kept], logs[:, buf, :]
                                  ).then_inc(kept_weights[buf], 16)

            def row_of_b(band, i, r):
                blocks = B.bands[band]
                tail = () if isinstance(r, int) and r == 0 else tail_b(r - 1)
                for k in range(len(blocks)):
                    inverse_square(B.before(band, i, k), k % 4)
                    for step, place in zip(tail, B_PLACES[len(blocks)]["act"]):
                        if place == k:
                            step()
                    last = earlier(B, band, i, k, 1)
                    if last:
                        weight(B, *last)

            def row_of_c(band, i, r):
                blocks = C.bands[band]
                start = isinstance(r, int) and r == 0
                tail = tail_b(G - 1) if start else tail_c(r - 1)
                if not start:
                    act.preload_act_table_set("natural_log_exp_and_others")
                for k, b in enumerate(blocks):
                    if b.weighed:
                        inverse_square(ALL_B + C.before(band, i, k, weighed), sum(x.weighed for x in blocks[:k]) % 4)
                    for step, place in zip(tail, (B_PLACES if start else C_PLACES)[len(blocks)]["act"]):
                        if place == k:
                            step()
                    if b.weighed or (band == LAST and isinstance(i, int) and k == 0):
                        d = 1
                        while True:
                            last = earlier(C, band, i, k, d)
                            if last is None or C.bands[last[0]][last[2]].weighed:
                                break
                            d += 1
                        if last:
                            weight(C, *last)
                        else:
                            weight(B, LAST, BAND - 1, G - 1)

            act.wait_ge(consts_set, 4)
            tanh_a(0)
            with act.Fori(1, G) as c:
                tanh_a(c)
            each_row(act, B, row_of_b)
            each_row(act, C, row_of_c)
            for step in tail_c(G - 1):
                step()


def kernel(x, adj, L0_gnn_W_stack, L0_gnn_B_stack, L1_gnn_W, L1_gnn_B):
    import numpy as np
    import concourse.bacc as bacc
    from concourse.bass_utils import run_bass_kernel_spmd

    x, adj = np.asarray(x), np.asarray(adj)
    n = adj.shape[0]
    groups = n // ROW
    blocks = np.ascontiguousarray(adj.reshape(groups, ROW, groups, T, P).transpose(0, 2, 4, 3, 1))
    arrays = {
        "x": np.ascontiguousarray(x),
        "x_t": np.ascontiguousarray(x.T),
        "adj": blocks,
        "w_stack": np.ascontiguousarray(L0_gnn_W_stack),
        "b_stack": np.ascontiguousarray(L0_gnn_B_stack),
        "w_msg": np.ascontiguousarray(L1_gnn_W),
        "bias_msg": np.ascontiguousarray(np.asarray(L1_gnn_B).reshape(1, -1)),
    }
    nc = bacc.Bacc("TRN2", target_bir_lowering=False, num_devices=1)
    args = [nc.dram_tensor(k, v.shape, mybir.dt.from_np(v.dtype), kind="ExternalInput").ap()
            for k, v in arrays.items()]
    out = nc.dram_tensor("out", x.shape, mybir.dt.from_np(x.dtype), kind="ExternalOutput").ap()
    graph_kernel(nc, *args, out)
    return run_bass_kernel_spmd(nc, [arrays], core_ids=[0]).results[0]["out"]
```

```python
from collections import namedtuple
from contextlib import ExitStack

import concourse.bass as bass
from concourse import mybir

P = 128
D = 128
ROW = 512
T = ROW // P
RING = 4
BAND = 4
EPS = 1e-5
LAG = 3
TINY = 1e-15


Block = namedtuple("Block", "g layer1 layer2 weighed summed kept buf half")


def every(b):
    return True


def layer1(b):
    return b.layer1


def direct(b):
    return b.layer1 or b.layer2 or not b.weighed


def weighed(b):
    return b.weighed


def summed(b):
    return b.weighed and b.summed


def stored(buf):
    return lambda b: b.weighed and b.kept is not None and b.buf == buf


class Pass:

    def __init__(self, prior, bands):
        self.prior, self.bands = prior, []
        for blocks in bands:
            done = []
            for b in blocks:
                done.append(b._replace(buf=sum(map(weighed, done)) % 4, half=sum(map(summed, done)) % 2))
            assert sum(map(weighed, done)) % 4 == sum(map(summed, done)) % 2 == len(done) % RING == 0
            self.bands.append(done)

    def before(self, band, i, k=0, which=every):
        rows = [[which(b) for b in blocks] for blocks in self.bands]
        n = BAND * sum(map(sum, rows[:band])) + sum(rows[band][:k]) + (self.prior.total(which) if self.prior else 0)
        return n + i * sum(rows[band]) if sum(rows[band]) else n

    def total(self, which=every):
        return self.before(len(self.bands) - 1, BAND, 0, which)


class Place:

    def __init__(self, table, band, i, k):
        self.table, self.band, self.i, self.k = table, band, i, k
        self.blocks = table.bands[band]
        self.block, self.row = self.blocks[k], band * BAND + i

    def before(self, which=every):
        return self.table.before(self.band, self.i, self.k, which)

    def through(self, which=every):
        return self.before(which) + 1

    def last_of_row(self, which=every):
        return not any(map(which, self.blocks[self.k + 1:]))

    def earlier(self, d=1, which=every):
        table, band, i, k = self.table, self.band, self.i, self.k
        while d:
            k -= 1
            if k < 0:
                if not isinstance(i, int) or i > 0:
                    i = i - 1
                else:
                    band, i = band - 1, BAND - 1
                if band < 0:
                    table = table.prior
                    if table is None:
                        return None
                    band = len(table.bands) - 1
                k = len(table.bands[band]) - 1
            d -= which(table.bands[band][k])
        return Place(table, band, i, k)


def ripe(place):
    last, other = place.earlier(1), place.earlier(2)
    if last and weighed(last.block):
        return last if weighed(place.block) else None
    return other if other and weighed(other.block) else None


def spread(few, many):
    count, total = len(few), len(few) + len(many)
    few, many = iter(few), iter(many)
    return [next(few if k * count % total < count else many) for k in range(total)]


def passes(groups):
    lows = range(0, groups, BAND)

    def kept_in(lo):
        if lo == 0:
            return [*range(BAND - 1, -1, -1)], False
        few = 2 * BAND if lo >= 2 * BAND else BAND
        return [*range(lo + BAND - 1, lo + BAND - 1 - few, -1)], True

    def block(lo, g, layer1=False, layer2=False, weighed=False, summed=False):
        kept = kept_in(lo)[0]
        return Block(g, layer1, layer2, weighed, summed, kept.index(g) if g in kept else None, 0, 0)

    up, down, rest = [], [], []
    for lo in lows:
        kept, in_a = kept_in(lo)
        few = [block(lo, g, layer1=True, layer2=g < lo, weighed=in_a) for g in kept]
        many = [block(lo, g, layer1=True, layer2=g < lo) for g in [*range(lo, groups), *range(lo)] if g not in kept]
        up.append(spread(few, many))
    for lo in reversed(lows):
        kept, in_a = kept_in(lo)
        own, others = range(lo, lo + BAND), range(groups - 1, lo + BAND - 1, -1)
        down.append(spread([block(lo, g, layer2=True, weighed=not in_a and g in kept) for g in own],
                           [block(lo, g, layer2=True, weighed=True, summed=True)._replace(kept=None)
                            for g in others]))
        rest.append(spread([block(lo, g, summed=True) for g in kept],
                           [block(lo, g, summed=True, weighed=True)
                            for g in range(lo + BAND - 1, -1, -1) if g not in kept]))
    a = Pass(None, up)
    b = Pass(a, down)
    return a, b, Pass(b, rest)


def each_row(engine, table, row):
    def places(band, i):
        return [Place(table, band, i, k) for k in range(len(table.bands[band]))]

    for band in range(len(table.bands)):
        single = 1 if band else 2
        for i in range(single):
            row(places(band, i), band * BAND + i)
        with engine.Fori(single, BAND) as i:
            row(places(band, i), band * BAND + i)


A_PLACES = {n: dict(dve=(1, 3), pe=(1, 2), act=(1,)) for n in (8, 16)}
AB_PLACES = dict(pe=(1, 2))
B_PLACES = {
    4: dict(dve=(0, 0, 0, 1, 1, 2), pe=(0, 1, 1), act=(0, 0)),
    8: dict(dve=(0, 3, 3, 4, 5, 6), pe=(0, 4, 5), act=(1, 3)),
    12: dict(dve=(0, 3, 4, 6, 8, 9), pe=(1, 7, 8), act=(2, 5)),
    16: dict(dve=(0, 3, 5, 7, 9, 11), pe=(1, 8, 10), act=(2, 6)),
}
C_PLACES = {
    4: dict(dve=(3, 3, 3), pe=(2,), act=(3,)),
    8: dict(dve=(3, 5, 7), pe=(4,), act=(6,)),
    12: dict(dve=(5, 8, 10), pe=(6,), act=(9,)),
    16: dict(dve=(5, 9, 11), pe=(6,), act=(10,)),
}


def run_steps(tail, places, k):
    for step, place in zip(tail, places):
        if place == k:
            step()


class Steps:

    def __init__(self, engine, sem, base):
        self.engine, self.sem, self.base, self.n = engine, sem, base, 0

    def did(self, instruction):
        self.n += 1
        return instruction.then_inc(self.sem, 1)

    def settle(self):
        self.engine.wait_ge(self.sem, self.base + self.n)


def graph_kernel(nc: bass.Bass, x, x_t, adj, w_stack, b_stack, w_msg, bias_msg, out):
    dt = mybir.dt
    f32, bf16, u32 = dt.float32, dt.bfloat16, dt.uint32
    ALU, ACT = mybir.AluOpType, mybir.ActivationFunctionType

    G = x.shape[0] // ROW
    A, B, C = passes(G)
    inv_deg_d = nc.dram_tensor("inv_deg_d", (G, P, ROW), f32, kind="Internal").ap()
    agg_d = nc.dram_tensor("agg_d", (G, P, ROW), f32, kind="Internal").ap()
    z1t_d = nc.dram_tensor("z1t_d", (G, P, ROW), f32, kind="Internal").ap()
    sum_d = nc.dram_tensor("sum_d", (G, P, ROW), f32, kind="Internal").ap()
    weights_d = nc.dram_tensor("weights_d", (G, 2 * BAND, P, T * ROW), f32, kind="Internal").ap()
    x1_d = nc.dram_tensor("x1_d", (G, P, T, D), f32, kind="Internal").ap()

    x_rows = x.rearrange("(c t p) d -> c p t d", t=T, p=P)
    out_rows = out.rearrange("(c t p) d -> c p t d", t=T, p=P)
    x_tiles = x.rearrange("(g p) d -> p g d", p=P)
    x_t_rows = x_t.rearrange("d (c n) -> c d n", n=ROW)

    ctx = ExitStack()
    with ctx:
        def sb(name, shape, dtype=f32):
            return ctx.enter_context(nc.sbuf_tensor(name, shape, dtype))

        def pb(name, shape):
            return ctx.enter_context(nc.psum_tensor(name, shape, f32))

        def sem(name):
            return ctx.enter_context(nc.semaphore(name))

        x_msg = sb("x_msg", [P, G * T, D])
        z1_nat = sb("z1_nat", [P, G * T, D])
        ring = sb("ring", [P, RING, T, ROW])
        masked = sb("masked", [P, 2, T * ROW])
        logs = sb("logs", [P, 4, T * ROW])
        weights = sb("weights", [P, 2, T * ROW])
        nonzero = sb("nonzero", [P, 2, T * ROW], bf16)
        ones_b = sb("ones_b", [P, P], bf16)
        ident = sb("ident", [P, P])
        w0, w1, b0, b1, wm = (sb(n, [P, D]) for n in ("w0", "w1", "b0", "b1", "wm"))
        bias = sb("bias", [P, T, D])
        tiny_c = sb("tiny_c", [P, 1])
        minus2_c = sb("minus2_c", [P, 1])
        inv_t = sb("inv_t", [P, ROW])
        deg_t = sb("deg_t", [P, ROW])
        part_t = sb("part_t", [P, ROW])
        agg_t = sb("agg_t", [P, ROW])
        side_t = sb("side_t", [P, ROW])
        tanh_t = sb("tanh_t", [P, ROW])
        sum_t = sb("sum_t", [P, ROW])
        res_t = sb("res_t", [P, T, D])
        pre_t = sb("pre_t", [P, T, D])
        norm_t = sb("norm_t", [P, T, D])
        x1t_t = sb("x1t_t", [P, T, P])
        stats = sb("stats", [P, T, 6])
        mean_var = sb("mean_var", [P, T, 2])
        var_eps, ln_var, rstd0, newton, rstd = (
            sb(n, [P, T]) for n in ("var_eps", "ln_var", "rstd0", "newton", "rstd"))

        acc_p = pb("acc_p", [P, 2, ROW])
        acc_q = pb("acc_q", [P, 2, ROW])
        deg_p = pb("deg_p", [P, ROW])
        pre_p = pb("pre_p", [P, ROW])
        turn_p = pb("turn_p", [P, T, P])
        msg_p = pb("msg_p", [P, T, D])

        consts_in, consts_set, ident_set = map(sem, ("consts_in", "consts_set", "ident_set"))
        bias_in = sem("bias_in")
        x_in = [sem(f"x_in{q}") for q in range(4)]
        adj_in = [sem(f"adj_in{k}") for k in range(RING)]
        adj_pe = sem("adj_pe")
        counted = sem("counted")
        mask_done = sem("mask_done")
        abs_done, ln_done, square_done = map(sem, ("abs_done", "ln_done", "square_done"))
        exponent_done, weight_done = map(sem, ("exponent_done", "weight_done"))
        weight_read = sem("weight_read")
        kept_weights = [sem(f"kept_weights{k}") for k in range(4)]
        ta_pe, ta_dve, ta_act = map(sem, ("ta_pe", "ta_dve", "ta_act"))
        tb_pe, tb_dve, tb_act = map(sem, ("tb_pe", "tb_dve", "tb_act"))
        tc_pe, tc_dve, tc_act = map(sem, ("tc_pe", "tc_dve", "tc_act"))
        side_a, side_b, side_c = map(sem, ("side_a", "side_b", "side_c"))
        kept_inv, kept_agg, kept_z1, kept_sum, kept_x1, kept_out = map(
            sem, ("kept_inv", "kept_agg", "kept_z1", "kept_sum", "kept_x1", "kept_out"))

        A_PE, A_DVE, A_ACT = 3, 5, 1
        A_AGG, A_Z1 = 4, 5
        NORM = 1 + T + T + 1
        FINISH = 3 + T
        B_PE, B_ACT = 3, 3
        B_AGG, B_SUM, B_VAR = 2, 3, 3 + NORM
        B_X1 = B_VAR + 1 + FINISH
        B_X1T, B_MSG = B_X1 + 1, B_X1 + 2
        B_DVE = B_MSG
        C_PE, C_ACT = 1, 2
        C_SUM, C_VAR = 1, 1 + NORM
        C_OUT = C_DVE = C_VAR + 1 + FINISH

        def apart(engine):
            engine.sem_inc(passed[engine], 1)

        def landed(place):
            in_slot = place.table.before(place.band, 0) // RING + place.k // RING + 1
            return 16 * (place.i * (len(place.blocks) // RING) + in_slot)

        passed = {nc.sync: sem("passed_sp"), nc.gpsimd: sem("passed_pool"), nc.vector: sem("passed_dve"),
                  nc.scalar: sem("passed_act")}

        block = ctx.enter_context(nc.Block())

        @block.sync
        def _(sp):
            quarter = G * T // 4

            def load(place, c):
                last = place.earlier(RING)
                if last:
                    if direct(last.block):
                        sp.wait_ge(adj_pe, last.through(direct))
                        apart(sp)
                    if layer1(last.block):
                        sp.wait_ge(counted, last.through(layer1))
                        apart(sp)
                    if weighed(last.block):
                        sp.wait_ge(mask_done, last.through(weighed))
                        apart(sp)
                slot, b = place.k % RING, place.block
                if place.table is C and not b.weighed:
                    sp.dma_start(ring[:, slot].rearrange("p t n -> p (t n)"), weights_d[c, b.kept]
                                 ).then_inc(adj_in[slot], 16)
                else:
                    sp.dma_start(ring[:, slot], adj[c, b.g]).then_inc(adj_in[slot], 16)

            def load_x(q):
                tiles = slice(q * quarter, (q + 1) * quarter)
                sp.dma_start(x_msg[:, tiles, :], x_tiles[:, tiles, :]).then_inc(x_in[q], 16)

            load_x(0)
            for tile, src in ((w0, w_stack[0]), (b0, b_stack[0]), (w1, w_stack[1]),
                              (b1, b_stack[1]), (wm, w_msg)):
                sp.dma_start(tile[:, :], src).then_inc(consts_in, 16)
            for t in range(T):
                sp.dma_start(bias[:, t, :], bias_msg[0].partition_broadcast(P)).then_inc(bias_in, 16)

            def load_row_a(places, r):
                for place in places:
                    load(place, r)
                    n = place.before()
                    if isinstance(n, int) and n < 3:
                        load_x(n + 1)

            def load_row_b(places, r):
                for place in places:
                    load(place, G - 1 - r)

            def load_row_c(places, r):
                if places[0].band == 0:
                    keeper = A if isinstance(r, int) and r == 0 else B
                    for buf in range(4):
                        sp.wait_ge(kept_weights[buf], 16 * keeper.total(stored(buf)))
                load_row_b(places, r)

            each_row(sp, A, load_row_a)
            each_row(sp, B, load_row_b)
            each_row(sp, C, load_row_c)

        @block.gpsimd
        def _(pool):
            pool.memset(ident[:, :], 0.0).then_inc(ident_set, 1)
            pool.wait_ge(ident_set, 1)
            pool.affine_select(out=ident[:, :], in_=ident[:, :], compare_op=ALU.not_equal, fill=1.0,
                               base=0, pattern=[[-1, P]], channel_multiplier=1).then_inc(ident_set, 1)

            def load_a(c):
                pool.dma_start(side_t[:, :], x_t_rows[c]).then_inc(side_a, 16)

            def load_b(c):
                pool.dma_start(part_t[:, :], agg_d[c]).then_inc(side_b, 16)
                pool.dma_start(inv_t[:, :], inv_deg_d[c]).then_inc(side_b, 16)
                pool.dma_start(side_t[:, :], z1t_d[c]).then_inc(side_b, 16)
                pool.dma_start(res_t[:, :, :], x_rows[c]).then_inc(side_b, 16)

            def load_c(c):
                pool.dma_start(part_t[:, :], sum_d[c]).then_inc(side_c, 16)
                pool.dma_start(res_t[:, :, :], x1_d[c]).then_inc(side_c, 16)

            def side_row_a(c, last=False):
                pool.wait_ge(ta_dve, c * A_DVE + A_AGG)
                apart(pool)
                pool.dma_start(inv_deg_d[c], inv_t[:, :]).then_inc(kept_inv, 16)
                pool.dma_start(agg_d[c], part_t[:, :]).then_inc(kept_agg, 16)
                if not last:
                    pool.wait_ge(ta_pe, c * A_PE + 2)
                    apart(pool)
                    load_a(c + 1)
                pool.wait_ge(ta_act, c * A_ACT + 1)
                apart(pool)
                pool.dma_start(z1t_d[c], tanh_t[:, :]).then_inc(kept_z1, 16)

            def side_row_b(r, last=False):
                c = G - 1 - r
                pool.wait_ge(tb_dve, r * B_DVE + B_SUM)
                apart(pool)
                pool.dma_start(sum_d[c], sum_t[:, :]).then_inc(kept_sum, 16)
                if not last:
                    pool.wait_ge(tb_pe, r * B_PE + 1)
                    apart(pool)
                    pool.wait_ge(tb_dve, r * B_DVE + B_SUM + 1)
                    apart(pool)
                    load_b(c - 1)
                pool.wait_ge(tb_dve, r * B_DVE + B_X1)
                apart(pool)
                pool.dma_start(x1_d[c], norm_t[:, :, :]).then_inc(kept_x1, 16)

            def side_row_c(r, last=False):
                c = G - 1 - r
                if not last:
                    pool.wait_ge(tc_dve, r * C_DVE + C_SUM + 1)
                    apart(pool)
                    load_c(c - 1)
                pool.wait_ge(tc_dve, r * C_DVE + C_OUT)
                apart(pool)
                pool.dma_start(out_rows[c], norm_t[:, :, :]).then_inc(kept_out, 16)

            def side_rows(side_row):
                with pool.Fori(0, G - 1) as r:
                    side_row(r)
                side_row(G - 1, last=True)

            load_a(0)
            side_rows(side_row_a)
            pool.wait_ge(ta_dve, G * A_DVE)
            pool.wait_ge(kept_inv, 16 * G)
            pool.wait_ge(kept_agg, 16 * G)
            pool.wait_ge(kept_z1, 16 * G)
            load_b(G - 1)
            side_rows(side_row_b)
            pool.wait_ge(tb_dve, G * B_DVE)
            pool.wait_ge(kept_sum, 16 * G)
            pool.wait_ge(kept_x1, 16 * G)
            load_c(G - 1)
            side_rows(side_row_c)
            pool.wait_ge(kept_out, 16 * G)

        @block.tensor
        def _(pe):
            def product(acc, stationary, moving, first, last):
                for t in range(T):
                    mm = pe.matmul(acc, stationary[:, t, :], moving[:, t, :],
                                   start=first and t == 0, stop=last and t == T - 1)
                return mm

            def tiles(z, g):
                return z[:, g * T:(g + 1) * T, :]

            def turn(steps, src):
                for t in range(T):
                    mm = pe.transpose(turn_p[:, t, :], src[:, t, :], ident[:, :])
                steps.did(mm)

            def tail_a(c):
                steps = Steps(pe, ta_pe, c * A_PE)

                def degree():
                    pe.wait_ge(counted, (c + 1) * G)
                    for t in range(T):
                        mm = pe.matmul(deg_p[:, :], ones_b[:, :], nonzero[:, c % 2, t * ROW:(t + 1) * ROW],
                                       start=t == 0, stop=t == T - 1)
                    steps.did(mm)

                def layer():
                    pe.wait_ge(ta_dve, c * A_DVE + A_AGG)
                    pe.wait_ge(side_a, (c + 1) * 16)
                    pe.matmul(pre_p[:, :], w0[:, :], agg_t[:, :], start=True, stop=False)
                    steps.did(pe.matmul(pre_p[:, :], b0[:, :], side_t[:, :], start=False, stop=True))

                def turn_z1():
                    pe.wait_ge(ta_act, c * A_ACT + 1)
                    turn(steps, tanh_t[:, :].rearrange("d (t p) -> d t p", p=P))

                return degree, layer, turn_z1

            def tail_b(r):
                steps = Steps(pe, tb_pe, r * B_PE)

                def layer():
                    pe.wait_ge(tb_dve, r * B_DVE + B_AGG)
                    pe.wait_ge(side_b, (r + 1) * 64)
                    for t in range(T):
                        rows = slice(t * P, (t + 1) * P)
                        pe.matmul(pre_p[:, rows], agg_t[:, rows], w1[:, :], start=True, stop=False)
                        mm = pe.matmul(pre_p[:, rows], side_t[:, rows], b1[:, :], start=False, stop=True)
                    steps.did(mm)

                def turn_x1():
                    pe.wait_ge(tb_dve, r * B_DVE + B_X1)
                    turn(steps, norm_t)

                def messages():
                    pe.wait_ge(tb_dve, r * B_DVE + B_X1T)
                    for t in range(T):
                        mm = pe.matmul(msg_p[:, t, :], x1t_t[:, t, :], wm[:, :], start=True, stop=True)
                    steps.did(mm)

                return layer, turn_x1, messages

            def tail_c(r):
                steps = Steps(pe, tc_pe, r * C_PE)

                def turn_sum():
                    pe.wait_ge(tc_dve, r * C_DVE + C_SUM)
                    turn(steps, sum_t[:, :].rearrange("d (t p) -> d t p", p=P))

                return (turn_sum,)

            def row_of_a(places, r):
                start = isinstance(r, int) and r == 0
                degree, *tail = tail_a(r - 1)
                if not start:
                    degree()
                second = [p.k for p in places if p.block.layer2]
                for place in places:
                    k, b, last = place.k, place.block, place.last_of_row()
                    if start:
                        pe.wait_ge(x_in[b.g // (G // 4)], 16)
                    pe.wait_ge(adj_in[k % RING], landed(place))
                    mm = product(acc_p[:, r % 2, :], tiles(x_msg, b.g), ring[:, k % RING], k == 0, last)
                    if b.layer2:
                        pe.wait_ge(ta_dve, (b.g + 1) * A_DVE)
                        mm = product(acc_q[:, r % 2, :], tiles(z1_nat, b.g), ring[:, k % RING],
                                     k == second[0], k == second[-1])
                    mm.then_inc(adj_pe, 1)
                    if not start:
                        run_steps(tail, A_PLACES[len(places)]["pe"], k)

            def sum_messages(place):
                b = place.block
                if not summed(b):
                    return
                if place.table is C:
                    acc, first = acc_p, False
                else:
                    acc, first = acc_q, not any(map(summed, place.blocks[:place.k]))
                pe.wait_ge(tb_dve, (G - b.g) * B_DVE)
                pe.wait_ge(weight_done, place.through(weighed))
                mm = product(acc[:, place.row % 2, :], tiles(x_msg, b.g),
                             weights[:, b.half, :].rearrange("p (t n) -> p t n", t=T),
                             first, place.last_of_row(summed))
                mm.then_inc(weight_read, 1)

            def row_of_b(places, r):
                if isinstance(r, int) and r == 0:
                    degree, *tail = tail_a(G - 1)
                    degree()
                    at = AB_PLACES["pe"]
                else:
                    tail, at = tail_b(r - 1), B_PLACES[len(places)]["pe"]
                for place in places:
                    k, b = place.k, place.block
                    pe.wait_ge(adj_in[k % RING], landed(place))
                    pe.wait_ge(ta_dve, (b.g + 1) * A_DVE)
                    mm = product(acc_p[:, r % 2, :], tiles(z1_nat, b.g), ring[:, k % RING],
                                 k == 0, place.last_of_row())
                    mm.then_inc(adj_pe, 1)
                    sum_messages(place.earlier(LAG))
                    run_steps(tail, at, k)

            def row_of_c(places, r):
                start = isinstance(r, int) and r == 0
                tail = tail_b(G - 1) if start else tail_c(r - 1)
                for place in places:
                    k, b = place.k, place.block
                    if not b.weighed:
                        pe.wait_ge(adj_in[k % RING], landed(place))
                        if start:
                            pe.wait_ge(tb_dve, (G - b.g) * B_DVE)
                        mm = product(acc_p[:, r % 2, :], tiles(x_msg, b.g), ring[:, k % RING],
                                     k == 0, place.last_of_row() and not any(map(summed, place.blocks)))
                        mm.then_inc(adj_pe, 1)
                    sum_messages(place.earlier(LAG))
                    run_steps(tail, (B_PLACES if start else C_PLACES)[len(places)]["pe"], k)

            pe.wait_ge(consts_in, 5 * 16)
            pe.wait_ge(consts_set, 3)
            pe.wait_ge(ident_set, 2)
            each_row(pe, A, row_of_a)
            each_row(pe, B, row_of_b)
            each_row(pe, C, row_of_c)
            for step in tail_c(G - 1):
                step()

        @block.vector
        def _(dve):
            def norm_stats(steps, source, source_sem, source_value, side_sem, side_value):
                dve.wait_ge(source_sem, source_value)
                dve.wait_ge(side_sem, side_value)
                steps.did(dve.tensor_tensor(out=pre_t[:, :, :], in0=source, in1=res_t[:, :, :], op=ALU.add))
                steps.settle()
                for t in range(T):
                    steps.did(dve.bn_stats(out=stats[:, t, :], in_=pre_t[:, t, :]))
                steps.settle()
                apart(dve)
                for t in range(T):
                    steps.did(dve.bn_aggr(out=mean_var[:, t, :], in_=stats[:, t, :]))
                steps.settle()
                steps.did(dve.tensor_scalar(var_eps[:, :], mean_var[:, :, 1], EPS, None, ALU.add))

            def norm_finish(steps, act_sem, act_value, kept, kept_value):
                dve.wait_ge(act_sem, act_value)
                steps.did(dve.tensor_tensor(out=newton[:, :], in0=rstd0[:, :], in1=rstd0[:, :], op=ALU.mult))
                steps.settle()
                steps.did(dve.tensor_tensor(out=newton[:, :], in0=newton[:, :], in1=var_eps[:, :], op=ALU.mult))
                steps.settle()
                steps.did(dve.tensor_scalar(newton[:, :], newton[:, :], -0.5, 1.5, ALU.mult, ALU.add))
                steps.settle()
                steps.did(dve.tensor_tensor(out=rstd[:, :], in0=newton[:, :], in1=rstd0[:, :], op=ALU.mult))
                steps.settle()
                if kept_value is not None:
                    dve.wait_ge(kept, kept_value)
                for t in range(T):
                    steps.did(dve.tensor_scalar(norm_t[:, t, :], pre_t[:, t, :], mean_var[:, t, 0:1],
                                                rstd[:, t:t + 1], ALU.subtract, ALU.mult))

            def tail_a(c, partial):
                steps = Steps(dve, ta_dve, c * A_DVE)
                first = isinstance(c, int) and c == 0

                def aggregate():
                    dve.wait_ge(ta_pe, c * A_PE + 1)
                    dve.wait_ge(adj_pe, (c + 1) * G)
                    if not first:
                        dve.wait_ge(kept_inv, c * 16)
                        dve.wait_ge(kept_agg, c * 16)
                    steps.did(dve.tensor_scalar(deg_t[:, :], deg_p[:, :], 1.0, None, ALU.max))
                    if partial:
                        steps.did(dve.tensor_copy(part_t[:, :], acc_q[:, c % 2, :]))
                    else:
                        steps.did(dve.memset(part_t[:, :], 0.0))
                    steps.settle()
                    steps.did(dve.reciprocal(inv_t[:, :], deg_t[:, :]))
                    steps.settle()
                    steps.did(dve.tensor_tensor(out=agg_t[:, :], in0=acc_p[:, c % 2, :], in1=inv_t[:, :], op=ALU.mult))

                def keep_z1():
                    dve.wait_ge(ta_pe, c * A_PE + 3)
                    apart(dve)
                    steps.did(dve.tensor_copy(z1_nat[:, bass.ds(c * T, T), :], turn_p[:, :, :]))

                return aggregate, keep_z1

            def tail_b(r, partial, blocks, sums):
                steps = Steps(dve, tb_dve, r * B_DVE)
                first = isinstance(r, int) and r == 0

                def aggregate():
                    dve.wait_ge(adj_pe, blocks)
                    dve.wait_ge(side_b, (r + 1) * 64)
                    steps.did(dve.tensor_tensor(out=agg_t[:, :], in0=acc_p[:, r % 2, :], in1=part_t[:, :], op=ALU.add))
                    steps.settle()
                    steps.did(dve.tensor_tensor(out=agg_t[:, :], in0=agg_t[:, :], in1=inv_t[:, :], op=ALU.mult))

                def partial_sum():
                    if not first:
                        dve.wait_ge(kept_sum, r * 16)
                    if partial:
                        dve.wait_ge(weight_read, sums)
                        steps.did(dve.tensor_copy(sum_t[:, :], acc_q[:, r % 2, :]))
                    else:
                        steps.did(dve.memset(sum_t[:, :], 0.0))

                def norm_in():
                    z2 = tanh_t[:, :].rearrange("p (t d) -> p t d", d=D)
                    norm_stats(steps, z2, tb_act, r * B_ACT + 1, side_b, (r + 1) * 64)

                def norm_out():
                    norm_finish(steps, tb_act, r * B_ACT + 3, kept_x1, None if first else r * 16)

                def keep_x1t():
                    dve.wait_ge(tb_pe, r * B_PE + 2)
                    steps.did(dve.tensor_copy(x1t_t[:, :, :], turn_p[:, :, :]))

                def keep_messages():
                    dve.wait_ge(tb_pe, r * B_PE + 3)
                    apart(dve)
                    steps.did(dve.tensor_tensor(out=x_msg[:, bass.ds((G - 1 - r) * T, T), :], in0=msg_p[:, :, :],
                                                in1=bias[:, :, :], op=ALU.add))
                    assert steps.n == B_DVE

                return aggregate, partial_sum, norm_in, norm_out, keep_x1t, keep_messages

            def tail_c(r, sums, kept):
                steps = Steps(dve, tc_dve, r * C_DVE)
                first = isinstance(r, int) and r == 0

                def whole_sum():
                    dve.wait_ge(weight_read, sums)
                    dve.wait_ge(adj_pe, kept)
                    dve.wait_ge(side_c, (r + 1) * 32)
                    if first:
                        dve.wait_ge(kept_sum, G * 16)
                    steps.did(dve.tensor_tensor(out=sum_t[:, :], in0=acc_p[:, r % 2, :], in1=part_t[:, :], op=ALU.add))

                def norm_in():
                    norm_stats(steps, turn_p[:, :, :], tc_pe, r * C_PE + 1, side_c, (r + 1) * 32)

                def norm_out():
                    norm_finish(steps, tc_act, r * C_ACT + 2, kept_x1 if first else kept_out,
                                G * 16 if first else r * 16)
                    assert steps.n == C_DVE

                return whole_sum, norm_in, norm_out

            def mask(place):
                l, buf, slot = place.before(weighed), place.block.buf, place.k % RING
                dve.wait_ge(adj_in[slot], landed(place))
                if not (isinstance(l, int) and l < 2):
                    dve.wait_ge(exponent_done, l - 1)
                r = ring[:, slot].rearrange("p t n -> p (t n)")
                dve.scalar_tensor_tensor(out=masked[:, buf % 2, :], in0=r, scalar=1.0, in1=r,
                                         op0=ALU.is_lt, op1=ALU.mult).then_inc(mask_done, 1)
                dve.wait_ge(mask_done, l + 1)
                last = place.earlier(4, weighed)
                if last and last.block.weighed and stored(buf)(last.block):
                    dve.wait_ge(kept_weights[buf], 16 * last.through(stored(buf)))
                elif last:
                    dve.wait_ge(weight_done, l - 3)
                dve.tensor_scalar(logs[:, buf, :].bitcast(u32), masked[:, buf % 2, :].bitcast(u32), 0x7FFFFFFF,
                                  None, ALU.bitwise_and).then_inc(abs_done, 1)

            def exponent(place):
                buf = place.block.buf
                dve.wait_ge(square_done, place.through(weighed))
                dve.scalar_tensor_tensor(out=logs[:, buf, :], in0=masked[:, buf % 2, :], scalar=-0.5,
                                         in1=logs[:, buf, :], op0=ALU.add, op1=ALU.mult
                                         ).then_inc(exponent_done, 1)

            def weigh(place):
                if weighed(place.block):
                    mask(place)
                if ripe(place):
                    exponent(ripe(place))

            def row_of_a(places, r):
                tail = ()
                if not (isinstance(r, int) and r == 0):
                    tail = tail_a(r - 1, places[0].earlier().band > 0)
                for place in places:
                    weigh(place)
                    k = place.k
                    dve.wait_ge(adj_in[k % RING], landed(place))
                    seen = ring[:, k % RING].rearrange("p t n -> p (t n)")
                    counts = nonzero[:, r % 2, :]
                    if k == 0:
                        dve.tensor_scalar(counts, seen, 0.0, None, ALU.not_equal).then_inc(counted, 1)
                    else:
                        dve.wait_ge(counted, place.before())
                        dve.scalar_tensor_tensor(out=counts, in0=seen, scalar=0.0, in1=counts,
                                                 op0=ALU.not_equal, op1=ALU.add).then_inc(counted, 1)
                    run_steps(tail, A_PLACES[len(places)]["dve"], k)

            def row_of_b(places, r):
                tail = ()
                if not (isinstance(r, int) and r == 0):
                    tail = tail_b(r - 1, places[0].earlier().band > 0,
                                  places[0].before(direct), places[0].before(summed))
                for place in places:
                    weigh(place)
                    run_steps(tail, B_PLACES[len(places)]["dve"], place.k)

            def row_of_c(places, r):
                counts = places[0].before(summed), places[0].before(direct)
                if isinstance(r, int) and r == 0:
                    tail, at = tail_b(G - 1, True, *reversed(counts)), B_PLACES[len(places)]["dve"]
                else:
                    tail, at = tail_c(r - 1, *counts), C_PLACES[len(places)]["dve"]
                for place in places:
                    weigh(place)
                    run_steps(tail, at, place.k)

            dve.memset(ones_b[:, :], 1.0).then_inc(consts_set, 1)
            dve.memset(tiny_c[:, :], TINY).then_inc(consts_set, 1)
            dve.memset(minus2_c[:, :], -2.0).then_inc(consts_set, 1)
            each_row(dve, A, row_of_a)
            for step in tail_a(G - 1, True):
                step()
            dve.wait_ge(bias_in, T * 16)
            each_row(dve, B, row_of_b)
            each_row(dve, C, row_of_c)
            for step in tail_c(G - 1, C.total(summed), C.total(direct)):
                step()

        @block.scalar
        def _(act):
            def tanh_a(c):
                act.wait_ge(ta_pe, c * A_PE + 2)
                if not (isinstance(c, int) and c == 0):
                    act.wait_ge(kept_z1, c * 16)
                act.activation(tanh_t[:, :], pre_p[:, :], ACT.Tanh).then_inc(ta_act, 1)
                act.preload_act_table_set("natural_log_exp_and_others")

            def root(dve_sem, dve_value, own, own_value):
                act.wait_ge(dve_sem, dve_value)
                act.activation(ln_var[:, :], var_eps[:, :], ACT.Ln).then_inc(own, 1)
                act.wait_ge(own, own_value + 1)
                act.activation(rstd0[:, :], ln_var[:, :], ACT.Exp, scale=-0.5).then_inc(own, 1)

            def tail_b(r):
                def tanh_b():
                    act.wait_ge(tb_pe, r * B_PE + 1)
                    if isinstance(r, int) and r == 0:
                        act.wait_ge(kept_z1, G * 16)
                    act.activation(tanh_t[:, :], pre_p[:, :], ACT.Tanh).then_inc(tb_act, 1)
                    act.preload_act_table_set("natural_log_exp_and_others")

                def root_b():
                    root(tb_dve, r * B_DVE + B_VAR, tb_act, r * B_ACT + 1)

                return [tanh_b, root_b]

            def tail_c(r):
                return [lambda: root(tc_dve, r * C_DVE + C_VAR, tc_act, r * C_ACT)]

            def inverse_square(place):
                l, buf = place.before(weighed), place.block.buf
                act.wait_ge(abs_done, l + 1)
                act.activation(logs[:, buf, :], logs[:, buf, :], ACT.Ln, bias=tiny_c[:, :]).then_inc(ln_done, 1)
                act.wait_ge(ln_done, l + 1)
                act.activation(logs[:, buf, :], logs[:, buf, :], ACT.Exp, scale=-2.0).then_inc(square_done, 1)

            def weight(place):
                b, l = place.block, place.before(weighed)
                act.wait_ge(exponent_done, l + 1)
                if b.summed:
                    s = place.before(summed)
                    if not (isinstance(s, int) and s < 2):
                        act.wait_ge(weight_read, s - 1)
                    act.activation(weights[:, b.half, :], logs[:, b.buf, :], ACT.Exp, bias=minus2_c[:, :],
                                   scale=4.0).then_inc(weight_done, 1)
                else:
                    act.activation(logs[:, b.buf, :], logs[:, b.buf, :], ACT.Exp, bias=minus2_c[:, :],
                                   scale=4.0).then_inc(weight_done, 1)
                    act.wait_ge(weight_done, l + 1)
                    apart(act)
                    c = place.row if place.table is A else G - 1 - place.row
                    act.dma_start(weights_d[c, b.kept], logs[:, b.buf, :]).then_inc(kept_weights[b.buf], 16)

            def row(places, tail, at):
                for place in places:
                    if weighed(place.block):
                        inverse_square(place)
                    run_steps(tail, at[len(places)]["act"], place.k)
                    if ripe(place):
                        weight(ripe(place))

            def row_of_a(places, r):
                row(places, () if isinstance(r, int) and r == 0 else [lambda: tanh_a(r - 1)], A_PLACES)

            def row_of_b(places, r):
                row(places, () if isinstance(r, int) and r == 0 else tail_b(r - 1), B_PLACES)

            def row_of_c(places, r):
                if isinstance(r, int) and r == 0:
                    row(places, tail_b(G - 1), B_PLACES)
                else:
                    act.preload_act_table_set("natural_log_exp_and_others")
                    row(places, tail_c(r - 1), C_PLACES)

            act.wait_ge(consts_set, 3)
            each_row(act, A, row_of_a)
            tanh_a(G - 1)
            each_row(act, B, row_of_b)
            each_row(act, C, row_of_c)
            for step in tail_c(G - 1):
                step()


def kernel(x, adj, L0_gnn_W_stack, L0_gnn_B_stack, L1_gnn_W, L1_gnn_B):
    import numpy as np
    import concourse.bacc as bacc
    from concourse.bass_utils import run_bass_kernel_spmd

    x, adj = np.asarray(x), np.asarray(adj)
    n = adj.shape[0]
    groups = n // ROW
    blocks = np.ascontiguousarray(adj.reshape(groups, ROW, groups, T, P).transpose(0, 2, 4, 3, 1))
    arrays = {
        "x": np.ascontiguousarray(x),
        "x_t": np.ascontiguousarray(x.T),
        "adj": blocks,
        "w_stack": np.ascontiguousarray(L0_gnn_W_stack),
        "b_stack": np.ascontiguousarray(L0_gnn_B_stack),
        "w_msg": np.ascontiguousarray(L1_gnn_W),
        "bias_msg": np.ascontiguousarray(np.asarray(L1_gnn_B).reshape(1, -1)),
    }
    nc = bacc.Bacc("TRN2", target_bir_lowering=False, num_devices=1)
    args = [nc.dram_tensor(k, v.shape, mybir.dt.from_np(v.dtype), kind="ExternalInput").ap()
            for k, v in arrays.items()]
    out = nc.dram_tensor("out", x.shape, mybir.dt.from_np(x.dtype), kind="ExternalOutput").ap()
    graph_kernel(nc, *args, out)
    return run_bass_kernel_spmd(nc, [arrays], core_ids=[0]).results[0]["out"]
```
